# Optimizing a Trainium2 kernel written in Bass

```python
import numpy as np
import jax
import jax.numpy as jnp

def _softmax(x, axis=-1):
    return jax.nn.softmax(x, axis=axis)
def _gelu(x):
    return jax.nn.gelu(x, approximate=True)
def _silu(x):
    return jax.nn.silu(x)
def _sigmoid(x):
    return jax.nn.sigmoid(x)
def _layernorm(x, axis=-1, eps=1e-5):
    m = jnp.mean(x, axis=axis, keepdims=True)
    v = jnp.var(x, axis=axis, keepdims=True)
    return (x - m) / jnp.sqrt(v + eps)
def _scatter_add(tgt, idx, src, axis=0):
    return tgt.at[idx].add(src)
def _segment_sum(src, seg, n):
    return jax.ops.segment_sum(src, seg, n)

kernel_name = 'mk_conv_preact_d1_conv_nhwc768_f6c100'

def setup_inputs(seed: int = 0):
    np.random.seed(seed)
    _w = jnp.asarray
    def _rec_inputs():
        import jax
        import jax.numpy as jnp
        _gk = jax.random.key(seed)
        x = -0.0001538 + 1 * jax.random.normal(jax.random.fold_in(_gk, 1), (8, 32, 32, 768), jnp.float32)
        return x
    x = _rec_inputs()
    def _L0_conv_setup():
        import jax, jax.numpy as jnp
        import numpy as np

        def rotate_every_two(x):
            x1 = x[..., ::2]
            x2 = x[..., 1::2]
            return jnp.stack([-x2, x1], axis=-1).reshape(x.shape)

        def theta_shift(x, sin, cos):
            return x * cos + rotate_every_two(x) * sin
        key = jax.random.key(seed)
        ks = jax.random.split(key, 16)
        B, H, W, C, NH = (8, 32, 32, 768, 12)
        HD = C // NH
        gain = 2 ** (-2.5)
        xavier = lambda k, shp, g: jax.random.normal(k, shp, jnp.float32) * (g * (2.0 / (shp[0] + shp[1])) ** 0.5)
        return {'x': jax.random.normal(ks[0], (B, H, W, C), jnp.float32), 'sin': jax.random.normal(ks[1], (H, W, HD), jnp.float32), 'cos': jax.random.normal(ks[2], (H, W, HD), jnp.float32), 'mask': jax.random.normal(ks[3], (NH, H * W, H * W), jnp.float32), 'wq': xavier(ks[4], (C, C), gain), 'bq': jnp.zeros((C,), jnp.float32), 'wk': xavier(ks[5], (C, C), gain), 'bk': jnp.zeros((C,), jnp.float32), 'wv': xavier(ks[6], (C, C), gain), 'bv': jnp.zeros((C,), jnp.float32), 'lepe_w': jax.random.normal(ks[7], (5, 5, 1, C), jnp.float32) * 0.05, 'lepe_b': jnp.zeros((C,), jnp.float32), 'wo': xavier(ks[8], (C, C), 1.0), 'bo': jnp.zeros((C,), jnp.float32)}
    _L0_conv_all = _L0_conv_setup()
    _L0_conv_in = {k: v for k, v in _L0_conv_all.items() if k in ('sin', 'cos', 'mask', 'wq', 'bq', 'wk', 'bk', 'wv', 'bv', 'lepe_w', 'lepe_b', 'wo', 'bo', )}
    del _L0_conv_all

    return {
        "x": x,
        "L0_conv_sin": _L0_conv_in["sin"],
        "L0_conv_cos": _L0_conv_in["cos"],
        "L0_conv_mask": _L0_conv_in["mask"],
        "L0_conv_wq": _L0_conv_in["wq"],
        "L0_conv_bq": _L0_conv_in["bq"],
        "L0_conv_wk": _L0_conv_in["wk"],
        "L0_conv_bk": _L0_conv_in["bk"],
        "L0_conv_wv": _L0_conv_in["wv"],
        "L0_conv_bv": _L0_conv_in["bv"],
        "L0_conv_lepe_w": _L0_conv_in["lepe_w"],
        "L0_conv_lepe_b": _L0_conv_in["lepe_b"],
        "L0_conv_wo": _L0_conv_in["wo"],
        "L0_conv_bo": _L0_conv_in["bo"],
    }

def reference(x, L0_conv_sin, L0_conv_cos, L0_conv_mask, L0_conv_wq, L0_conv_bq, L0_conv_wk, L0_conv_bk, L0_conv_wv, L0_conv_bv, L0_conv_lepe_w, L0_conv_lepe_b, L0_conv_wo, L0_conv_bo):
    import jax
    import jax.numpy as jnp
    def _L0_conv_ref(x, sin, cos, mask, wq, bq, wk, bk, wv, bv, lepe_w, lepe_b, wo, bo):
        import jax, jax.numpy as jnp
        import numpy as np

        def rotate_every_two(x):
            x1 = x[..., ::2]
            x2 = x[..., 1::2]
            return jnp.stack([-x2, x1], axis=-1).reshape(x.shape)

        def theta_shift(x, sin, cos):
            return x * cos + rotate_every_two(x) * sin
        B, H, W, C = x.shape
        NH = mask.shape[0]
        scaling = (C // NH) ** (-0.5)
        q = x @ wq.T + bq
        k = (x @ wk.T + bk) * scaling
        v = x @ wv.T + bv
        lepe = jax.lax.conv_general_dilated(v, lepe_w, window_strides=(1, 1), padding=[(2, 2), (2, 2)], dimension_numbers=('NHWC', 'HWIO', 'NHWC'), feature_group_count=C) + lepe_b
        qh = q.reshape(B, H, W, NH, -1).transpose(0, 3, 1, 2, 4)
        kh = k.reshape(B, H, W, NH, -1).transpose(0, 3, 1, 2, 4)
        qr = theta_shift(qh, sin, cos).reshape(B, NH, H * W, -1)
        kr = theta_shift(kh, sin, cos).reshape(B, NH, H * W, -1)
        vr = v.reshape(B, H, W, NH, -1).transpose(0, 3, 1, 2, 4).reshape(B, NH, H * W, -1)
        qk = jnp.einsum('bnld,bnmd->bnlm', qr, kr) + mask
        attn = jax.nn.softmax(qk, axis=-1)
        out = jnp.einsum('bnlm,bnmd->bnld', attn, vr)
        out = jnp.swapaxes(out, 1, 2).reshape(B, H, W, -1) + lepe
        return out @ wo.T + bo

    def _gn(v, G=32, eps=1e-5):
        B_, H_, W_, C_ = v.shape
        g = v.reshape(B_, H_, W_, G, C_ // G)
        m = jnp.mean(g, axis=(1, 2, 4), keepdims=True)
        s = jnp.var(g, axis=(1, 2, 4), keepdims=True)
        return ((g - m) / jnp.sqrt(s + eps)).reshape(v.shape)

    def _ln_c(v, eps=1e-6):
        m = jnp.mean(v, axis=-1, keepdims=True)
        s = jnp.var(v, axis=-1, keepdims=True)
        return (v - m) / jnp.sqrt(s + eps)

    def _ln_t(v, eps=1e-5):
        m = jnp.mean(v, axis=-1, keepdims=True)
        s = jnp.var(v, axis=-1, keepdims=True)
        return (v - m) / jnp.sqrt(s + eps)

    def _to_tokens(v):
        B_, H_, W_, C_ = v.shape
        return v.reshape(B_, H_ * W_, C_)
    def _from_tokens(t, like):
        return t.reshape(like.shape)

    x = x + _L0_conv_ref(_gn(x), L0_conv_sin, L0_conv_cos, L0_conv_mask, L0_conv_wq, L0_conv_bq, L0_conv_wk, L0_conv_bk, L0_conv_wv, L0_conv_bv, L0_conv_lepe_w, L0_conv_lepe_b, L0_conv_wo, L0_conv_bo)
    return x


_drawn_inputs = setup_inputs


def setup_inputs(seed=0):
    import zlib

    import numpy as np

    out = dict(_drawn_inputs(seed))
    spreads = {'L0_conv_bq': (0.0, 0.8),
     'L0_conv_bk': (0.0, 0.8),
     'L0_conv_bv': (0.0, 0.1),
     'L0_conv_lepe_b': (0.0, 0.1),
     'L0_conv_bo': (0.0, 0.1)}
    factors = {'L0_conv_sin': 8.0, 'L0_conv_cos': 8.0, 'L0_conv_wq': 8.0, 'L0_conv_wk': 8.0}
    for name, (base, spread) in spreads.items():
        noise = np.random.default_rng([zlib.crc32(name.encode()), seed]).standard_normal(out[name].shape)
        drawn = base * np.exp(spread * noise) if base else spread * noise
        out[name] = jnp.asarray(drawn.astype(out[name].dtype))
    for name, factor in factors.items():
        out[name] = (out[name] * factor).astype(out[name].dtype)
    return out
```

```python
import concourse.bass as bass
from concourse import mybir
from contextlib import ExitStack

B, SIDE, C, NH = 8, 32, 768, 12
L = SIDE * SIDE
HD = C // NH
P = 128
NT = C // P
HALF = 512
NK = L // P
NQ = 2 * NK
KS = 5
PAD = KS // 2
PSIDE = SIDE + 2 * PAD
TAPS = KS * KS
GROUPS = 32
W_SCALE = 256.0
P_SCALE = 4096.0
GN_EPS = 1e-5
BIG = 3.0e38
FREE = 1
COL_LB, COL_K, COL_Q, COL_V, COL_O, NCOL = TAPS, TAPS + 1, TAPS + 2, TAPS + 3, TAPS + 4, TAPS + 5


def conv_preact(nc, xt, w3, wo, cols_in, mask, sin_in, cos_in, ident_in, gavg_in, sign_in, out, w_scr, x_scr):
    fp32, fp16 = mybir.dt.float32, mybir.dt.float16
    ALU, ACT = mybir.AluOpType, mybir.ActivationFunctionType

    with ExitStack() as top:
        wo_sb = top.enter_context(nc.sbuf_tensor("wo_sb", [P, NT, 2, C], fp16))
        prepare(nc, xt, w3, wo, gavg_in, w_scr, x_scr, wo_sb, fp32, fp16, ALU, ACT)
        main(nc, xt, cols_in, mask, sin_in, cos_in, ident_in, sign_in, out, w_scr, x_scr, wo_sb, fp32, fp16, ALU, ACT)


def prepare(nc, xt, w3, wo, gavg_in, w_scr, x_scr, wo_sb, fp32, fp16, ALU, ACT):
    with ExitStack() as ctx:
        def sb(name, shape, dt):
            return ctx.enter_context(nc.sbuf_tensor(name, shape, dt))

        def sem(name):
            return ctx.enter_context(nc.semaphore(name))

        wraw = sb("wraw", [P, 2, 3 * NT * P], fp32)
        wsplit = sb("wsplit", [P, 2, 3 * NT, 2, P], fp16)
        woraw = sb("woraw", [P, NT, C], fp32)
        gavg = sb("gavg", [P, NT, C], fp32)
        xs = sb("xs", [P, 2, NT, L], fp32)
        xsplit = sb("xsplit", [P, 2, NT, 2, L], fp16)
        bn = sb("bn", [P, NT, 2, 6], fp32)
        st = sb("st", [P, NT, 2], fp32)
        dev = sb("dev", [P, NT], fp32)
        tot = sb("tot", [P, NT], fp32)
        var = sb("var", [P, NT], fp32)
        sd = sb("sd", [P, NT], fp32)
        rs = sb("rs", [P, NT], fp32)
        nt1 = sb("nt1", [P, NT], fp32)
        nt2 = sb("nt2", [P, NT], fp32)
        rstd = sb("rstd", [P, NT], fp32)
        shift = sb("shift", [P, NT], fp32)
        mean_ps = ctx.enter_context(nc.psum_tensor("mean_ps", [P, HALF], fp32))
        var_ps = ctx.enter_context(nc.psum_tensor("var_ps", [P, HALF], fp32))
        eps = sb("eps", [P, 1], fp32)

        w_in = [sem(f"w_in{n}") for n in range(2)]
        w_out = [sem(f"w_out{n}") for n in range(2)]
        wo_in = sem("wo_in")
        gavg_ok = sem("gavg_ok")
        w_hi = sem("w_hi")
        w_lo = sem("w_lo")
        x_in = [sem(f"x_in{n}") for n in range(2)]
        x_out = [sem(f"x_out{n}") for n in range(2)]
        stored = sem("stored")
        x_last = sem("x_last")
        eps_ok = sem("eps_ok")
        bn_ok = sem("bn_ok")
        st_ok = sem("st_ok")
        mean_ok = sem("mean_ok")
        small = sem("small")
        tot_ok = sem("tot_ok")
        var_ok = sem("var_ok")
        sd_ok = sem("sd_ok")
        aff_ok = sem("aff_ok")
        xn_ok = sem("xn_ok")
        xhi_ok = sem("xhi_ok")
        xlo_ok = sem("xlo_ok")
        gate = sem("gate")
        SMALL = 11

        block = ctx.enter_context(nc.Block())

        @block.sync
        def _(sp):
            for j in range(2):
                sp.dma_start(wraw[:, j, :], w3[j]).then_inc(w_in[j], 16)
            for u in range(2):
                sp.dma_start(xs[:, u], xt[u]).then_inc(x_in[u], 16)
            sp.dma_start(gavg[:], gavg_in).then_inc(gavg_ok, 16)
            for j in range(2, NT):
                sp.wait_ge(w_lo, j - 1)
                sp.dma_start(wraw[:, j % 2, :], w3[j]).then_inc(w_in[j % 2], 16)
            sp.dma_start(woraw[:], wo).then_inc(wo_in, 16)
            with sp.Fori(1, B // 2) as it:
                for u in range(2):
                    sp.wait_ge(xlo_ok, (it * 2 + (u - 1)) * NT)
                    sp.dma_start(xs[:, u], xt[it * 2 + u]).then_inc(x_in[u], 16)

        @block.gpsimd
        def _(pool):
            for j in range(NT):
                pool.wait_ge(w_lo, j + 1)
                pool.dma_start(w_scr[j], wsplit[:, j % 2]).then_inc(w_out[j % 2], 16)
            with pool.Fori(0, B // 2) as it:
                for u in range(2):
                    pool.wait_ge(xlo_ok, (it * 2 + (u + 1)) * NT)
                    pool.sem_inc(gate, 1)
                    pool.dma_start(x_scr[it * 2 + u], xsplit[:, u]).then_inc(x_out[u], 16)
                    pool.wait_ge(x_out[u], it * 16 + 16)
                    pool.sem_inc(stored, 1)
            pool.dma_start(x_scr[B], xsplit[:, 1]).then_inc(x_last, 16)
            pool.wait_ge(x_last, 16)
            for u in range(2):
                pool.wait_ge(w_out[u], 16 * (NT // 2))

        @block.scalar
        def _(act):
            for j in range(NT):
                act.wait_ge(w_in[j % 2], 16 * (j // 2 + 1))
                if j >= 2:
                    act.wait_ge(w_out[j % 2], 16 * (j // 2))
                nc.scalar.activation(wsplit[:, j % 2, :, 0, :], wraw[:, j % 2, :].rearrange("p (k o) -> p k o", o=P),
                                     ACT.Copy, scale=W_SCALE).then_inc(w_hi, 1)
            act.wait_ge(wo_in, 16)
            nc.scalar.activation(wo_sb[:, :, 0, :], woraw[:], ACT.Copy, scale=W_SCALE).then_inc(w_hi, 1)
            act.wait_ge(eps_ok, 1)
            with act.Fori(0, B // 2) as it:
                for u in range(2):
                    q = it * 2 + u
                    act.wait_ge(var_ok, q + 1)
                    nc.scalar.activation(sd[:], var_ps[:, 0:NT], ACT.Sqrt, bias=eps[:, 0:1]).then_inc(sd_ok, 1)
                    act.wait_ge(aff_ok, q + 1)
                    for c in range(NT):
                        nc.scalar.activation(xs[:, u, c, :], xs[:, u, c, :], ACT.Identity, bias=shift[:, c:c + 1],
                                             scale=rstd[:, c:c + 1]).then_inc(xn_ok, 1)
                    for c in range(NT):
                        act.wait_ge(xn_ok, q * NT + (c + 1))
                        if c == 0:
                            act.wait_ge(stored, q + 1)
                        nc.scalar.activation(xsplit[:, u, c, 0, :], xs[:, u, c, :], ACT.Copy).then_inc(xhi_ok, 1)

        @block.tensor
        def _(pe):
            pe.wait_ge(gavg_ok, 16)
            with pe.Fori(0, B // 2) as it:
                for u in range(2):
                    q = it * 2 + u
                    for dst, src, ready, done in ((mean_ps, st[:, :, 0], st_ok, mean_ok), (var_ps, tot, tot_ok, var_ok)):
                        pe.wait_ge(ready, q + 1)
                        for m in range(NT):
                            near = [k for k in range(NT) if k // 3 == m // 3]
                            for k in near:
                                last = nc.tensor.matmul(dst[:, m:m + 1], gavg[:, k, m * P:(m + 1) * P],
                                                        src[:, k:k + 1], start=(k == near[0]), stop=(k == near[-1]))
                        last.then_inc(done, 1)

        @block.vector
        def _(dve):
            dve.sem_inc(small, FREE)
            dve.sem_inc(stored, 2)
            nc.vector.memset(eps[:], GN_EPS).then_inc(eps_ok, 1)
            for j in range(NT):
                dve.wait_ge(w_hi, j + 1)
                nc.vector.scalar_tensor_tensor(
                    wsplit[:, j % 2, :, 1, :], wraw[:, j % 2, :].rearrange("p (k o) -> p k o", o=P), W_SCALE,
                    wsplit[:, j % 2, :, 0, :], ALU.mult, ALU.subtract).then_inc(w_lo, 1)
            dve.wait_ge(w_hi, NT + 1)
            nc.vector.scalar_tensor_tensor(wo_sb[:, :, 1, :], woraw[:], W_SCALE, wo_sb[:, :, 0, :],
                                           ALU.mult, ALU.subtract).then_inc(w_lo, 1)
            with dve.Fori(0, B // 2) as it:
                for u in range(2):
                    q = it * 2 + u
                    dve.wait_ge(x_in[u], it * 16 + 16)
                    dve.wait_ge(small, q * SMALL + FREE)
                    for c in range(NT):
                        for h in range(2):
                            nc.vector.bn_stats(bn[:, c, h, :], xs[:, u, c, h * HALF:(h + 1) * HALF]).then_inc(bn_ok, 1)
                    dve.wait_ge(bn_ok, q * 2 * NT + 2 * NT)
                    dve.sem_inc(gate, 1)
                    for c in range(NT):
                        last = nc.vector.bn_aggr(st[:, c, :], bn[:, c, :, :])
                        if c < NT - 1:
                            last.then_inc(small, 1)
                    last.then_inc(st_ok, 1)
                    base = q * SMALL + (NT - 1)
                    dve.wait_ge(mean_ok, q + 1)
                    nc.vector.tensor_tensor(dev[:], st[:, :, 0], mean_ps[:, 0:NT], ALU.subtract).then_inc(small, 1)
                    dve.wait_ge(small, base + 1 + FREE)
                    nc.vector.tensor_tensor(nt1[:], dev[:], dev[:], ALU.mult).then_inc(small, 1)
                    dve.wait_ge(small, base + 2 + FREE)
                    nc.vector.tensor_tensor(tot[:], nt1[:], st[:, :, 1], ALU.add).then_inc(tot_ok, 1)
                    dve.wait_ge(var_ok, q + 1)
                    dve.wait_ge(sd_ok, q + 1)
                    nc.vector.tensor_scalar(var[:], var_ps[:, 0:NT], GN_EPS, -0.5, ALU.add, ALU.mult)
                    nc.vector.reciprocal(rs[:], sd[:]).then_inc(small, 1)
                    dve.wait_ge(small, base + 3 + FREE)
                    nc.vector.tensor_tensor(nt1[:], rs[:], rs[:], ALU.mult).then_inc(small, 1)
                    dve.wait_ge(small, base + 4 + FREE)
                    nc.vector.tensor_tensor(nt2[:], nt1[:], var[:], ALU.mult).then_inc(small, 1)
                    dve.wait_ge(small, base + 5 + FREE)
                    nc.vector.scalar_tensor_tensor(rstd[:], nt2[:], 1.5, rs[:], ALU.add, ALU.mult).then_inc(small, 1)
                    dve.wait_ge(small, base + 6 + FREE)
                    nc.vector.scalar_tensor_tensor(shift[:], mean_ps[:, 0:NT], -1.0, rstd[:], ALU.mult,
                                                   ALU.mult).then_inc(aff_ok, 1)
                    for c in range(NT):
                        dve.wait_ge(xhi_ok, q * NT + (c + 1))
                        nc.vector.tensor_tensor(xsplit[:, u, c, 1, :], xs[:, u, c, :], xsplit[:, u, c, 0, :],
                                                ALU.subtract).then_inc(xlo_ok, 1)


def main(nc, xt, cols_in, mask, sin_in, cos_in, ident_in, sign_in, out, w_scr, x_scr, wo_sb, fp32, fp16, ALU, ACT):
    with ExitStack() as ctx:
        def sb(name, shape, dt):
            return ctx.enter_context(nc.sbuf_tensor(name, shape, dt))

        def pb(name, shape, dt):
            return ctx.enter_context(nc.psum_tensor(name, shape, dt))

        def sem(name):
            return ctx.enter_context(nc.semaphore(name))

        cols = sb("cols", [P, NT, NCOL], fp32)
        pbias = sb("pbias", [P, NT, 3], fp32)
        biases = sb("biases", [P, 3], fp32)
        sin_sb = sb("sin_sb", [P, L], fp32)
        cos_sb = sb("cos_sb", [P, L], fp32)
        sign = sb("sign", [P, 1], fp32)
        ident = sb("ident", [P, P], fp32)
        xn = sb("xn", [P, NT, 2, L], fp16)
        w_sb = sb("w_sb", [P, 3, NT, 2, P], fp16)
        kq = sb("kq", [P, 2, L], fp32)
        kq_swap = sb("kq_swap", [P, 2, L], fp32)
        v_sb = sb("v_sb", [P, L], fp32)
        rot = sb("rot", [P, L], fp32)
        kq_hi = sb("kq_hi", [P, 2, L], fp16)
        kq_lo = sb("kq_lo", [P, 2, L], fp16)
        q_stack = sb("q_stack", [P, 2, L], fp16)
        k_hihi = sb("k_hihi", [P, 2, L], fp16)
        k_lolo = sb("k_lolo", [P, 2, L], fp16)
        v_nat = sb("v_nat", [P, NK, 2, 2, HD], fp16)
        mask_sb = sb("mask_sb", [P, 4, L], fp32)
        neg = sb("neg", [P, 2, L], fp32)
        neg_max = sb("neg_max", [P, NQ], fp32)
        rowsum = sb("rowsum", [P, NQ], fp32)
        rowrec = sb("rowrec", [P, NQ], fp32)
        prob = sb("prob", [P, 2, L], fp32)
        pt_hi = sb("pt_hi", [P, 2, L], fp16)
        pt_lo = sb("pt_lo", [P, 2, L], fp16)
        o_hi = sb("o_hi", [P, 2, 4, HD], fp32)
        o_sum = sb("o_sum", [P, 4, HD], fp32)
        o_nat = sb("o_nat", [P, NK, P], fp32)
        v_pad = sb("v_pad", [P, PSIDE, PSIDE], fp32)
        dw_cols = sb("dw_cols", [P, NCOL], fp32)
        dw = sb("dw", [P, L], fp32)
        o_split = sb("o_split", [P, NT, 2, L], fp16)
        x_res = sb("x_res", [P, 2, L], fp32)
        out_sb = sb("out_sb", [P, 2, L], fp32)

        ps = pb("ps", [P, 2, 2, HALF], fp32)
        pt = pb("pt", [P, 2, HALF], fp32)
        pv = pb("pv", [P, 2, 4, 2, HD], fp32)

        s_const = sem("s_const")
        s_ready = sem("s_ready")
        s_mask = [sem(f"s_mask{n}") for n in range(4)]
        s_w = sem("s_w")
        s_xn = sem("s_xn")
        s_proj = sem("s_proj")
        s_pev = sem("s_pev")
        s_bias = sem("s_bias")
        s_swap = [sem(f"s_swap{n}") for n in range(2)]
        s_rot = sem("s_rot")
        s_rhi = sem("s_rhi")
        s_rlo = sem("s_rlo")
        s_rmul = sem("s_rmul")
        s_rmul2 = sem("s_rmul2")
        s_kstack = sem("s_kstack")
        s_qstack = sem("s_qstack")
        s_vt = sem("s_vt")
        s_vhi = sem("s_vhi")
        s_vlo = sem("s_vlo")
        s_vpad = sem("s_vpad")
        s_cols = sem("s_cols")
        s_s = sem("s_s")
        s_min = sem("s_min")
        s_exp = sem("s_exp")
        s_t = sem("s_t")
        s_hi = sem("s_hi")
        s_lo = sem("s_lo")
        s_pv = sem("s_pv")
        s_ohi = sem("s_ohi")
        s_rec = sem("s_rec")
        s_osum = sem("s_osum")
        s_on = sem("s_on")
        s_dw = sem("s_dw")
        s_ot = sem("s_ot")
        s_ota = sem("s_ota")
        s_othi = sem("s_othi")
        s_otlo = sem("s_otlo")
        s_op = sem("s_op")
        s_oev = sem("s_oev")
        s_xr = [sem(f"s_xr{n}") for n in range(2)]
        s_res = sem("s_res")
        s_store = [sem(f"s_store{n}") for n in range(2)]
        s_gate = [sem(f"s_gate{n}") for n in range(2)]
        s_stored = sem("s_stored")
        NCONST = 6

        block = ctx.enter_context(nc.Block())

        def steps(eng, step, after):
            with eng.Fori(0, B) as b:
                with eng.Fori(0, NT - 1) as j:
                    step(b * NT + j, b, j, j + 1, False)
                step(b * NT + (NT - 1), b, NT - 1, 0, True)
                after(b)

        @block.sync
        def _(sp):
            sp.dma_start(cols[:], cols_in).then_inc(s_const, 16)
            sp.dma_start(w_sb[:], w_scr[0]).then_inc(s_w, 16)
            sp.dma_start(xn[:], x_scr[0]).then_inc(s_xn, 16)
            for dst, src in ((ident[:], ident_in), (sign[:], sign_in), (sin_sb[0:HD, :], sin_in), (sin_sb[HD:P, :], sin_in)):
                sp.dma_start(dst, src).then_inc(s_const, 16)
            for h in range(2):
                sp.dma_start(cos_sb[h * HD:(h + 1) * HD, :], cos_in).then_inc(s_const, 16)

            def turn(p):
                for n in range(2):
                    sp.wait_ge(s_pev, p * 6 + (2 * n + 2))
                    for o in range(2):
                        sp.dma_start(kq_swap[o:P:2, n, :], kq[1 - o:P:2, n, :]).then_inc(s_swap[n], 16)
                sp.wait_ge(s_rlo, p * 2 + 1)
                for h in range(2):
                    for r in range(2):
                        for dst, src in ((k_hihi, kq_hi), (k_lolo, kq_lo)):
                            sp.dma_start(dst[r * HD:(r + 1) * HD, h, :],
                                         src[h * HD:(h + 1) * HD, 0, :]).then_inc(s_kstack, 16)
                sp.wait_ge(s_rlo, p * 2 + 2)
                for h in range(2):
                    for r, src in enumerate((kq_hi, kq_lo)):
                        sp.dma_start(q_stack[r * HD:(r + 1) * HD, h, :],
                                     src[h * HD:(h + 1) * HD, 1, :]).then_inc(s_qstack, 16)

            turn(0)

            def step(t, b, j, jn, last):
                for i in range(NQ):
                    sp.wait_ge(s_min, t * NQ + max(i - 3, 0) + FREE)
                    sp.dma_start(mask_sb[:, i % 4, :], mask[j * 2 + i // NK, i % NK]).then_inc(s_mask[i % 4], 16)
                    if i == 3:
                        sp.wait_ge(s_proj, t * 6 + 6)
                        sp.dma_start(w_sb[:], w_scr[jn]).then_inc(s_w, 16)
                        if last:
                            sp.dma_start(xn[:], x_scr[b + 1]).then_inc(s_xn, 16)
                turn(t + 1)

            steps(sp, step, lambda b: None)
            sp.wait_ge(s_kstack, 128 * (B * NT + 1))
            sp.wait_ge(s_qstack, 64 * (B * NT + 1))

        @block.gpsimd
        def _(pool):
            with pool.Fori(0, B) as b:
                for m in range(2):
                    pool.wait_ge(s_res, b * 2 * NT + FREE)
                    pool.sem_inc(s_gate[1], 1)
                    pool.dma_start(x_res[:, m, :], xt[b, :, m, :]).then_inc(s_xr[m], 16)
                for m in range(NT):
                    pool.wait_ge(s_res, b * 2 * NT + (2 * m + 2) + FREE)
                    pool.sem_inc(s_gate[1], 1)
                    pool.dma_start(out[b, :, m, :], out_sb[:, m % 2, :]).then_inc(s_store[m % 2], 16)
                    if m + 2 < NT:
                        pool.dma_start(x_res[:, m % 2, :], xt[b, :, m + 2, :]).then_inc(s_xr[m % 2], 16)
                    pool.wait_ge(s_store[m % 2], b * (16 * NT // 2) + 16 * (m // 2 + 1))
                    pool.sem_inc(s_stored, 1)

        @block.scalar
        def _(act):
            act.wait_ge(s_ready, 4)

            def project(p, jn):
                nc.scalar.activation(biases[:], pbias[:, jn, :], ACT.Copy).then_inc(s_bias, 1)
                act.wait_ge(s_bias, p + 1)
                for a in range(4):
                    act.wait_ge(s_proj, p * 6 + (a + 1))
                    n, h = a // 2, a % 2
                    nc.scalar.activation(kq[:, n, h * HALF:(h + 1) * HALF], ps[:, n, h, :], ACT.Identity,
                                         bias=biases[:, n:n + 1],
                                         scale=(HD ** -0.5 if n == 0 else 1.0) / W_SCALE).then_inc(s_pev, 1)

                def high(n):
                    act.wait_ge(s_rot, p * 2 + (n + 1))
                    nc.scalar.activation(kq_hi[:, n, :], rot[:], ACT.Copy).then_inc(s_rhi, 1)

                high(0)
                for h in range(2):
                    act.wait_ge(s_proj, p * 6 + (5 + h))
                    nc.scalar.activation(v_sb[:, h * HALF:(h + 1) * HALF], ps[:, 0, h, :], ACT.Identity,
                                         bias=biases[:, 2:3], scale=1.0 / W_SCALE).then_inc(s_pev, 1)
                high(1)
                for h in range(2):
                    act.wait_ge(s_vt, p * 2 + (h + 1))
                    nc.scalar.activation(v_nat[:, 4 * h:4 * h + 4, :, 0, :],
                                         pt[:, h, :].rearrange("p (k h c) -> p k h c", k=4, h=2),
                                         ACT.Copy).then_inc(s_vhi, 1)

            def pad(n):
                nc.scalar.activation(v_pad[:, PAD:PAD + SIDE, PAD:PAD + SIDE],
                                     v_sb[:].rearrange("p (r c) -> p r c", c=SIDE), ACT.Copy).then_inc(s_vpad, 1)

            project(0, 0)
            act.wait_ge(s_pev, 6)
            pad(0)

            def step(t, b, j, jn, last):
                def high(i):
                    for h in range(2):
                        act.wait_ge(s_t, t * 2 * NQ + (2 * i + h + 1) + FREE)
                        if h == 0:
                            act.wait_ge(s_pv, t * NQ + max(i - 1, 0) + FREE)
                        nc.scalar.activation(pt_hi[:, i % 2, h * HALF:(h + 1) * HALF], pt[:, h, :], ACT.Copy,
                                             scale=P_SCALE).then_inc(s_hi, 1)

                def group(g):
                    act.wait_ge(s_pv, t * NQ + 4 * (g + 1) + FREE)
                    nc.scalar.activation(o_hi[:, g % 2], pv[:, g % 2, :, 0, :], ACT.Copy,
                                         scale=1.0 / P_SCALE).then_inc(s_ohi, 1)

                for i in range(NQ + 3):
                    if 1 <= i <= NQ:
                        high(i - 1)
                    if i >= 6 and (i - 6) % 4 == 0 and i < NQ + 2:
                        group((i - 6) // 4)
                    if i < NQ:
                        act.wait_ge(s_min, t * NQ + (i + 1) + FREE)
                        act.wait_ge(s_t, t * 2 * NQ + max(2 * (i - 1), 0) + FREE)
                        nc.scalar.activation(prob[:, i % 2, :], neg[:, i % 2, :], ACT.Exp, scale=-1.0,
                                             bias=neg_max[:, i:i + 1], accum_out=rowsum[:, i:i + 1]).then_inc(s_exp, 1)
                group(3)
                project(t + 1, jn)
                act.wait_ge(s_dw, t * TAPS + TAPS)
                act.wait_ge(s_ota, t * 2 + 2 + FREE)
                pad(t)
                nc.scalar.activation(o_split[:, j, 0, :], dw[:], ACT.Copy).then_inc(s_othi, 1)

            def after(b):
                for a in range(2 * NT):
                    m, h = a // 2, a % 2
                    act.wait_ge(s_op, b * 2 * NT + (a + 1))
                    if h == 0:
                        act.wait_ge(s_stored, b * NT + max(m - 1, 0) + FREE)
                    nc.scalar.activation(out_sb[:, m % 2, h * HALF:(h + 1) * HALF], ps[:, (a // 2) % 2, h, :],
                                         ACT.Identity, bias=cols[:, m, COL_O:COL_O + 1],
                                         scale=1.0 / W_SCALE).then_inc(s_oev, 1)

            steps(act, step, after)

        @block.tensor
        def _(pe):
            TERMS = ((0, 0), (0, 1), (1, 0))

            def project(p, b, first, last):
                pe.wait_ge(s_w, p * 16 + 16)
                if first:
                    pe.wait_ge(s_xn, 16)
                else:
                    pe.wait_ge(s_min, p * NQ + FREE)
                if last:
                    pe.wait_ge(s_xn, b * 16 + 32)
                for a in range(6):
                    n, h = a // 2, a % 2
                    if n == 2:
                        pe.wait_ge(s_pev, p * 6 + (h + 1))
                    for k in range(NT):
                        for s, m in TERMS:
                            mm = nc.tensor.matmul(ps[:, n % 2, h, :], w_sb[:, n, k, s, :],
                                                  xn[:, k, m, h * HALF:(h + 1) * HALF],
                                                  start=(k == 0 and (s, m) == TERMS[0]),
                                                  stop=(k == NT - 1 and (s, m) == TERMS[-1]))
                    mm.then_inc(s_proj, 1)
                for h in range(2):
                    pe.wait_ge(s_pev, p * 6 + (5 + h))
                    if not first:
                        pe.wait_ge(s_lo, p * 2 * NQ)
                    for k in range(4):
                        mm = nc.tensor.transpose(pt[:, h, k * P:(k + 1) * P],
                                                 v_sb[:, h * HALF + k * P:h * HALF + (k + 1) * P], ident[:])
                    mm.then_inc(s_vt, 1)

            pe.wait_ge(s_const, 16 * (NCONST + 1))
            project(0, 0, True, False)

            def step(t, b, j, jn, last):
                def scores(i):
                    h, q = i // NK, i % NK
                    if i == 0:
                        pe.wait_ge(s_kstack, t * 128 + 128)
                        pe.wait_ge(s_qstack, t * 64 + 64)
                        pe.wait_ge(s_pev, t * 6 + 6)
                        pe.wait_ge(s_oev, b * 2 * NT + FREE)
                    if i >= 2:
                        pe.wait_ge(s_min, t * NQ + (i - 1) + FREE)
                    for s, k_part in enumerate((k_hihi, k_lolo)):
                        for n in range(2):
                            mm = nc.tensor.matmul(ps[:, i % 2, n, :], q_stack[:, h, q * P:(q + 1) * P],
                                                  k_part[:, h, n * HALF:(n + 1) * HALF], start=(s == 0), stop=(s == 1))
                    mm.then_inc(s_s, 1)

                def transposes(i):
                    pe.wait_ge(s_exp, t * NQ + (i + 1) + FREE)
                    for h in range(2):
                        if i == 0:
                            pe.wait_ge(s_ota, t * 2 + FREE)
                            pe.wait_ge(s_vlo, t * 2 + 2)
                        else:
                            pe.wait_ge(s_lo, t * 2 * NQ + (2 * i - 1 + h))
                        for k in range(4):
                            c = (4 * h + k) * P
                            mm = nc.tensor.transpose(pt[:, h, k * P:(k + 1) * P], prob[:, i % 2, c:c + P], ident[:])
                        mm.then_inc(s_t, 1)

                def values(i):
                    h, g = i // NK, i // 4
                    if i % 4 == 0:
                        pe.wait_ge(s_on, t * 4 + max(g - 1, 0) + FREE)
                    pe.wait_ge(s_lo, t * 2 * NQ + (2 * i + 2))
                    for s, part in enumerate((pt_hi, pt_lo)):
                        for k in range(NK):
                            mm = nc.tensor.matmul(pv[:, g % 2, i % 4].rearrange("p a c -> p (a c)"),
                                                  part[:, i % 2, k * P:(k + 1) * P],
                                                  v_nat[:, k, h].rearrange("p a c -> p (a c)"),
                                                  start=(s == 0 and k == 0), stop=(s == 1 and k == NK - 1))
                    mm.then_inc(s_pv, 1)

                for i in range(NQ + 2):
                    if i < NQ:
                        scores(i)
                    if 1 <= i <= NQ:
                        transposes(i - 1)
                    if i >= 2:
                        values(i - 2)
                project(t + 1, b, False, last)
                pe.wait_ge(s_on, t * 4 + 4 + FREE)
                for h in range(2):
                    pe.wait_ge(s_vlo, t * 2 + (3 + h))
                    for k in range(4):
                        mm = nc.tensor.transpose(pt[:, h, k * P:(k + 1) * P], o_nat[:, 4 * h + k, :], ident[:])
                    mm.then_inc(s_ot, 1)

            def after(b):
                pe.wait_ge(s_otlo, b * NT + NT + FREE)
                pe.wait_ge(s_pev, b * 6 * NT + 6 * (NT + 1))
                for a in range(2 * NT):
                    m, h = a // 2, a % 2
                    if a >= 4:
                        pe.wait_ge(s_oev, b * 2 * NT + (a - 3) + FREE)
                    for k in range(NT):
                        for s, r in TERMS:
                            mm = nc.tensor.matmul(ps[:, m % 2, h, :], wo_sb[:, k, s, m * P:(m + 1) * P],
                                                  o_split[:, k, r, h * HALF:(h + 1) * HALF],
                                                  start=(k == 0 and (s, r) == TERMS[0]),
                                                  stop=(k == NT - 1 and (s, r) == TERMS[-1]))
                    mm.then_inc(s_op, 1)

            steps(pe, step, after)

        @block.vector
        def _(dve):
            for free in (s_min, s_res, s_pv, s_t, s_oev, s_ota, s_on, s_exp, s_othi, s_otlo, s_stored):
                dve.sem_inc(free, FREE)
            nc.vector.memset(v_pad[:], 0.0).then_inc(s_ready, 1)
            dve.wait_ge(s_const, 16 * (NCONST + 1))
            nc.vector.tensor_scalar(pbias[:, :, 0], cols[:, :, COL_K], HD ** -0.5, None, ALU.mult).then_inc(s_ready, 1)
            nc.vector.tensor_copy(pbias[:, :, 1:3], cols[:, :, COL_Q:COL_V + 1]).then_inc(s_ready, 1)
            nc.vector.tensor_scalar(sin_sb[:], sin_sb[:], sign[:, 0:1], None, ALU.mult).then_inc(s_ready, 1)
            dve.wait_ge(s_ready, 4)

            def rotate(p, n, taps):
                dve.wait_ge(s_pev, p * 6 + (2 * n + 2))
                if n == 1:
                    dve.wait_ge(s_rhi, p * 2 + 1)
                    dve.wait_ge(s_rlo, p * 2 + 1)
                nc.vector.tensor_tensor(rot[:], kq[:, n, :], cos_sb[:], ALU.mult).then_inc(s_rmul, 1)
                taps(1)
                dve.wait_ge(s_swap[n], p * 32 + 32)
                nc.vector.tensor_tensor(kq_swap[:, n, :], kq_swap[:, n, :], sin_sb[:], ALU.mult).then_inc(s_rmul2, 1)
                dve.wait_ge(s_rmul, p * 2 + (n + 1))
                dve.wait_ge(s_rmul2, p * 2 + (n + 1))
                nc.vector.tensor_tensor(rot[:], rot[:], kq_swap[:, n, :], ALU.add).then_inc(s_rot, 1)
                taps(1)
                dve.wait_ge(s_rhi, p * 2 + (n + 1))
                nc.vector.tensor_tensor(kq_lo[:, n, :], rot[:], kq_hi[:, n, :], ALU.subtract).then_inc(s_rlo, 1)

            def value_lows(p):
                for h in range(2):
                    dve.wait_ge(s_vhi, p * 2 + (h + 1))
                    nc.vector.tensor_tensor(v_nat[:, 4 * h:4 * h + 4, :, 1, :],
                                            pt[:, h, :].rearrange("p (k h c) -> p k h c", k=4, h=2),
                                            v_nat[:, 4 * h:4 * h + 4, :, 0, :], ALU.subtract).then_inc(s_vlo, 1)

            rotate(0, 0, lambda n: None)
            rotate(0, 1, lambda n: None)
            value_lows(0)

            def step(t, b, j, jn, last):
                done = [0]

                image = dw[:].rearrange("p (r c) -> p r c", c=SIDE)

                def taps(n):
                    for _ in range(n):
                        k = done[0]
                        if k >= TAPS:
                            return
                        r, c = k // KS, k % KS
                        src = v_pad[:, r:r + SIDE, c:c + SIDE]
                        if k == 0:
                            dve.wait_ge(s_vpad, t + 1)
                            dve.wait_ge(s_cols, t + 1)
                            dve.wait_ge(s_othi, t + FREE)
                            dve.wait_ge(s_otlo, t + FREE)
                            ins = nc.vector.tensor_scalar(image, src, dw_cols[:, 0:1], dw_cols[:, COL_LB:COL_LB + 1],
                                                          ALU.mult, ALU.add)
                        else:
                            dve.wait_ge(s_dw, t * TAPS + k)
                            ins = nc.vector.scalar_tensor_tensor(image, src, dw_cols[:, k:k + 1], image,
                                                                 ALU.mult, ALU.add)
                        ins.then_inc(s_dw, 1)
                        done[0] += 1

                def low(i):
                    for h in range(2):
                        dve.wait_ge(s_hi, t * 2 * NQ + (2 * i + h + 1))
                        nc.vector.scalar_tensor_tensor(pt_lo[:, i % 2, h * HALF:(h + 1) * HALF], pt[:, h, :], P_SCALE,
                                                       pt_hi[:, i % 2, h * HALF:(h + 1) * HALF],
                                                       ALU.mult, ALU.subtract).then_inc(s_lo, 1)

                def group(g):
                    h = g // 2
                    dve.wait_ge(s_ohi, t * 4 + (g + 1))
                    nc.vector.reciprocal(rowrec[:, 4 * g:4 * g + 4], rowsum[:, 4 * g:4 * g + 4]).then_inc(s_rec, 1)
                    nc.vector.scalar_tensor_tensor(o_sum[:], pv[:, g % 2, :, 1, :], 1.0 / P_SCALE, o_hi[:, g % 2],
                                                   ALU.mult, ALU.add).then_inc(s_osum, 1)
                    dve.wait_ge(s_rec, t * 4 + (g + 1))
                    dve.wait_ge(s_osum, t * 4 + (g + 1))
                    nc.vector.tensor_tensor(o_nat[:, 4 * (g % 2):4 * (g % 2) + 4, h * HD:(h + 1) * HD], o_sum[:],
                                            rowrec[:, 4 * g:4 * g + 4].unsqueeze(2).to_broadcast([P, 4, HD]),
                                            ALU.mult).then_inc(s_on, 1)

                nc.vector.tensor_copy(dw_cols[:], cols[:, j, :]).then_inc(s_cols, 1)
                for i in range(NQ + 3):
                    if i < NQ:
                        dve.wait_ge(s_s, t * NQ + (i + 1))
                        dve.wait_ge(s_exp, t * NQ + max(i - 1, 0) + FREE)
                        dve.wait_ge(s_mask[i % 4], t * 64 + 16 * (i // 4 + 1))
                        dve.sem_inc(s_gate[0], 1)
                        nc.vector.tensor_tensor_reduce(out=neg[:, i % 2, :], in0=ps[:, i % 2].rearrange("p a n -> p (a n)"),
                                                       in1=mask_sb[:, i % 4, :], scale=-1.0, scalar=BIG, op0=ALU.add,
                                                       op1=ALU.min, accum_out=neg_max[:, i:i + 1]).then_inc(s_min, 1)
                    if 1 <= i <= NQ:
                        low(i - 1)
                        taps(1)
                    if i >= 6 and (i - 6) % 4 == 0 and i < NQ + 2:
                        group((i - 6) // 4)
                group(3)
                p = t + 1
                taps(3)
                rotate(p, 0, taps)
                rotate(p, 1, taps)
                taps(TAPS)
                value_lows(p)
                for h in range(2):
                    dve.wait_ge(s_ot, t * 2 + (h + 1))
                    if h == 0:
                        dve.wait_ge(s_dw, t * TAPS + TAPS)
                        dve.wait_ge(s_otlo, t + FREE)
                    nc.vector.tensor_tensor(dw[:, h * HALF:(h + 1) * HALF], pt[:, h, :], dw[:, h * HALF:(h + 1) * HALF],
                                            ALU.add).then_inc(s_ota, 1)
                dve.wait_ge(s_othi, t + 1 + FREE)
                nc.vector.tensor_tensor(o_split[:, j, 1, :], dw[:], o_split[:, j, 0, :],
                                        ALU.subtract).then_inc(s_otlo, 1)

            def after(b):
                for a in range(2 * NT):
                    m, h = a // 2, a % 2
                    dve.wait_ge(s_oev, b * 2 * NT + (a + 1) + FREE)
                    dve.wait_ge(s_xr[m % 2], b * (16 * NT // 2) + 16 * (m // 2 + 1))
                    half = slice(h * HALF, (h + 1) * HALF)
                    nc.vector.tensor_tensor(out_sb[:, m % 2, half], out_sb[:, m % 2, half], x_res[:, m % 2, half],
                                            ALU.add).then_inc(s_res, 1)

            steps(dve, step, after)


def kernel(**inputs):
    import numpy as np
    import concourse.bacc as bacc
    from concourse.bass_utils import run_bass_kernel_spmd

    a = {k.removeprefix("L0_conv_"): np.asarray(v) for k, v in inputs.items()}
    tiles = lambda w: w.reshape(NT, P, NT, P).transpose(0, 3, 2, 1)
    lanes = lambda v: v.reshape(NT, P).T
    f = np.float32
    arrays = {
        "xt": a["x"].reshape(B, L, NT, P).transpose(0, 3, 2, 1),
        "w3": np.stack([tiles(a["wk"]), tiles(a["wq"]), tiles(a["wv"])], axis=2).reshape(NT, P, 3 * NT * P),
        "wo": a["wo"].T.reshape(NT, P, C).transpose(1, 0, 2),
        "cols": np.stack([lanes(t) for t in a["lepe_w"].reshape(TAPS, C)]
                         + [lanes(a[n]) for n in ("lepe_b", "bk", "bq", "bv", "bo")], axis=2),
        "mask": a["mask"].reshape(NH, NK, P, L),
        "sin": a["sin"].reshape(L, HD).T,
        "cos": a["cos"].reshape(L, HD).T,
        "ident": np.eye(P, dtype=f),
        "gavg": (np.equal.outer(np.arange(C) // (C // GROUPS), np.arange(C) // (C // GROUPS)).astype(f)
                 * f(GROUPS / C)).reshape(NT, P, C).transpose(1, 0, 2),
        "sign": np.where(np.arange(P) % 2 == 0, -1, 1).astype(f).reshape(P, 1),
    }
    arrays = {k: np.ascontiguousarray(v) for k, v in arrays.items()}
    nc = bacc.Bacc("TRN2", target_bir_lowering=False, num_devices=1)
    fp32, fp16 = mybir.dt.float32, mybir.dt.float16
    d = {k: nc.dram_tensor(f"{k}_in", v.shape, fp32, kind="ExternalInput").ap() for k, v in arrays.items()}
    out = nc.dram_tensor("out_t", (B, P, NT, L), fp32, kind="ExternalOutput").ap()
    w_scr = nc.dram_tensor("w_scr", (NT, P, 3, NT, 2, P), fp16, kind="Internal").ap()
    x_scr = nc.dram_tensor("x_scr", (B + 1, P, NT, 2, L), fp16, kind="Internal").ap()
    conv_preact(nc, d["xt"], d["w3"], d["wo"], d["cols"], d["mask"], d["sin"], d["cos"], d["ident"], d["gavg"],
                d["sign"], out, w_scr, x_scr)
    r = run_bass_kernel_spmd(nc, [{f"{k}_in": v for k, v in arrays.items()}], core_ids=[0])
    got = r.results[0]["out_t"]
    return np.ascontiguousarray(got.transpose(0, 3, 2, 1)).reshape(B, SIDE, SIDE, C)
```

```python
import concourse.bass as bass
from concourse import mybir
from contextlib import ExitStack

B, SIDE, C, NH = 8, 32, 768, 12
L = SIDE * SIDE
HD = C // NH
P = 128
NT = C // P
HALF = 512
NK = L // P
NQ = 2 * NK
KS = 5
PAD = KS // 2
PSIDE = SIDE + 2 * PAD
TAPS = KS * KS
POOL_TAPS = 14
DVE_TAPS = TAPS - POOL_TAPS
LAG = 2
LATE = 4
GROUPS = 32
W_SCALE = 256.0
P_SCALE = 4096.0
GN_EPS = 1e-5
BIG = 3.0e38
FREE = 1
COL_LB, COL_K, COL_Q, COL_V, COL_O, NCOL = TAPS, TAPS + 1, TAPS + 2, TAPS + 3, TAPS + 4, TAPS + 5


def conv_preact(nc, xt, w3, wo, cols_in, mask, sin_in, cos_in, ident_in, gavg_in, sign_in, out, w_scr, x_scr):
    fp32, fp16 = mybir.dt.float32, mybir.dt.float16
    ALU, ACT = mybir.AluOpType, mybir.ActivationFunctionType

    with ExitStack() as top:
        wo_sb = top.enter_context(nc.sbuf_tensor("wo_sb", [P, NT, 2, C], fp16))
        prepare(nc, xt, w3, wo, gavg_in, w_scr, x_scr, wo_sb, fp32, fp16, ALU, ACT)
        main(nc, xt, cols_in, mask, sin_in, cos_in, ident_in, sign_in, out, w_scr, x_scr, wo_sb, fp32, fp16, ALU, ACT)


def prepare(nc, xt, w3, wo, gavg_in, w_scr, x_scr, wo_sb, fp32, fp16, ALU, ACT):
    with ExitStack() as ctx:
        def sb(name, shape, dt):
            return ctx.enter_context(nc.sbuf_tensor(name, shape, dt))

        def sem(name):
            return ctx.enter_context(nc.semaphore(name))

        wraw = sb("wraw", [P, 2, 3 * NT * P], fp32)
        wsplit = sb("wsplit", [P, 2, 3 * NT, 2, P], fp16)
        woraw = sb("woraw", [P, NT, C], fp32)
        gavg = sb("gavg", [P, NT, C], fp32)
        xs = sb("xs", [P, 2, NT, L], fp32)
        xsplit = sb("xsplit", [P, 2, NT, 2, L], fp16)
        bn = sb("bn", [P, NT, 2, 6], fp32)
        st = sb("st", [P, NT, 2], fp32)
        dev = sb("dev", [P, NT], fp32)
        tot = sb("tot", [P, NT], fp32)
        var = sb("var", [P, NT], fp32)
        sd = sb("sd", [P, NT], fp32)
        rs = sb("rs", [P, NT], fp32)
        nt1 = sb("nt1", [P, NT], fp32)
        nt2 = sb("nt2", [P, NT], fp32)
        rstd = sb("rstd", [P, NT], fp32)
        shift = sb("shift", [P, NT], fp32)
        mean_ps = ctx.enter_context(nc.psum_tensor("mean_ps", [P, HALF], fp32))
        var_ps = ctx.enter_context(nc.psum_tensor("var_ps", [P, HALF], fp32))
        eps = sb("eps", [P, 1], fp32)

        w_in = [sem(f"w_in{n}") for n in range(2)]
        w_out = [sem(f"w_out{n}") for n in range(2)]
        w_again = [sem(f"w_again{n}") for n in range(2)]
        wo_in = sem("wo_in")
        gavg_ok = sem("gavg_ok")
        w_hi = sem("w_hi")
        w_lo = sem("w_lo")
        x_in = [sem(f"x_in{n}") for n in range(2)]
        x_out = [sem(f"x_out{n}") for n in range(2)]
        stored = sem("stored")
        x_last = sem("x_last")
        eps_ok = sem("eps_ok")
        bn_ok = sem("bn_ok")
        st_ok = sem("st_ok")
        mean_ok = sem("mean_ok")
        small = sem("small")
        tot_ok = sem("tot_ok")
        var_ok = sem("var_ok")
        sd_ok = sem("sd_ok")
        aff_ok = sem("aff_ok")
        xn_ok = sem("xn_ok")
        xhi_ok = sem("xhi_ok")
        xlo_ok = sem("xlo_ok")
        gate = sem("gate")
        SMALL = 11

        block = ctx.enter_context(nc.Block())

        @block.sync
        def _(sp):
            for j in range(2):
                sp.dma_start(wraw[:, j, :], w3[j]).then_inc(w_in[j], 16)
            for u in range(2):
                sp.dma_start(xs[:, u], xt[u]).then_inc(x_in[u], 16)
            sp.dma_start(gavg[:], gavg_in).then_inc(gavg_ok, 16)
            for j in range(2, NT):
                sp.wait_ge(w_lo, j - 1)
                sp.dma_start(wraw[:, j % 2, :], w3[j]).then_inc(w_in[j % 2], 16)
            sp.dma_start(woraw[:], wo).then_inc(wo_in, 16)
            with sp.Fori(1, B // 2) as it:
                for u in range(2):
                    sp.wait_ge(xlo_ok, (it * 2 + (u - 1)) * NT)
                    sp.dma_start(xs[:, u], xt[it * 2 + u]).then_inc(x_in[u], 16)

        @block.gpsimd
        def _(pool):
            for j in range(NT):
                pool.wait_ge(w_lo, j + 1)
                pool.dma_start(w_scr[j], wsplit[:, j % 2]).then_inc(w_out[j % 2], 16)
                if j < 2:
                    pool.dma_start(w_scr[NT + j], wsplit[:, j]).then_inc(w_again[j], 16)
            with pool.Fori(0, B // 2) as it:
                for u in range(2):
                    pool.wait_ge(xlo_ok, (it * 2 + (u + 1)) * NT)
                    pool.sem_inc(gate, 1)
                    pool.dma_start(x_scr[it * 2 + u], xsplit[:, u]).then_inc(x_out[u], 16)
                    pool.wait_ge(x_out[u], it * 16 + 16)
                    pool.sem_inc(stored, 1)
            pool.dma_start(x_scr[B], xsplit[:, 1]).then_inc(x_last, 16)
            pool.wait_ge(x_last, 16)
            for u in range(2):
                pool.wait_ge(w_out[u], 16 * (NT // 2))

        @block.scalar
        def _(act):
            for j in range(NT):
                act.wait_ge(w_in[j % 2], 16 * (j // 2 + 1))
                if j >= 2:
                    act.wait_ge(w_out[j % 2], 16 * (j // 2))
                if j in (2, 3):
                    act.wait_ge(w_again[j - 2], 16)
                nc.scalar.activation(wsplit[:, j % 2, :, 0, :], wraw[:, j % 2, :].rearrange("p (k o) -> p k o", o=P),
                                     ACT.Copy, scale=W_SCALE).then_inc(w_hi, 1)
            act.wait_ge(wo_in, 16)
            nc.scalar.activation(wo_sb[:, :, 0, :], woraw[:], ACT.Copy, scale=W_SCALE).then_inc(w_hi, 1)
            act.wait_ge(eps_ok, 1)
            with act.Fori(0, B // 2) as it:
                for u in range(2):
                    q = it * 2 + u
                    act.wait_ge(var_ok, q + 1)
                    nc.scalar.activation(sd[:], var_ps[:, 0:NT], ACT.Sqrt, bias=eps[:, 0:1]).then_inc(sd_ok, 1)
                    act.wait_ge(aff_ok, q + 1)
                    for c in range(NT):
                        nc.scalar.activation(xs[:, u, c, :], xs[:, u, c, :], ACT.Identity, bias=shift[:, c:c + 1],
                                             scale=rstd[:, c:c + 1]).then_inc(xn_ok, 1)
                    for c in range(NT):
                        act.wait_ge(xn_ok, q * NT + (c + 1))
                        if c == 0:
                            act.wait_ge(stored, q + 1)
                        nc.scalar.activation(xsplit[:, u, c, 0, :], xs[:, u, c, :], ACT.Copy).then_inc(xhi_ok, 1)

        @block.tensor
        def _(pe):
            pe.wait_ge(gavg_ok, 16)
            with pe.Fori(0, B // 2) as it:
                for u in range(2):
                    q = it * 2 + u
                    for dst, src, ready, done in ((mean_ps, st[:, :, 0], st_ok, mean_ok), (var_ps, tot, tot_ok, var_ok)):
                        pe.wait_ge(ready, q + 1)
                        for m in range(NT):
                            near = [k for k in range(NT) if k // 3 == m // 3]
                            for k in near:
                                last = nc.tensor.matmul(dst[:, m:m + 1], gavg[:, k, m * P:(m + 1) * P],
                                                        src[:, k:k + 1], start=(k == near[0]), stop=(k == near[-1]))
                        last.then_inc(done, 1)

        @block.vector
        def _(dve):
            dve.sem_inc(small, FREE)
            dve.sem_inc(stored, 2)
            nc.vector.memset(eps[:], GN_EPS).then_inc(eps_ok, 1)
            for j in range(NT):
                dve.wait_ge(w_hi, j + 1)
                nc.vector.scalar_tensor_tensor(
                    wsplit[:, j % 2, :, 1, :], wraw[:, j % 2, :].rearrange("p (k o) -> p k o", o=P), W_SCALE,
                    wsplit[:, j % 2, :, 0, :], ALU.mult, ALU.subtract).then_inc(w_lo, 1)
            dve.wait_ge(w_hi, NT + 1)
            nc.vector.scalar_tensor_tensor(wo_sb[:, :, 1, :], woraw[:], W_SCALE, wo_sb[:, :, 0, :],
                                           ALU.mult, ALU.subtract).then_inc(w_lo, 1)
            with dve.Fori(0, B // 2) as it:
                for u in range(2):
                    q = it * 2 + u
                    dve.wait_ge(x_in[u], it * 16 + 16)
                    dve.wait_ge(small, q * SMALL + FREE)
                    for c in range(NT):
                        for h in range(2):
                            nc.vector.bn_stats(bn[:, c, h, :], xs[:, u, c, h * HALF:(h + 1) * HALF]).then_inc(bn_ok, 1)
                    dve.wait_ge(bn_ok, q * 2 * NT + 2 * NT)
                    dve.sem_inc(gate, 1)
                    for c in range(NT):
                        last = nc.vector.bn_aggr(st[:, c, :], bn[:, c, :, :])
                        if c < NT - 1:
                            last.then_inc(small, 1)
                    last.then_inc(st_ok, 1)
                    base = q * SMALL + (NT - 1)
                    dve.wait_ge(mean_ok, q + 1)
                    nc.vector.tensor_tensor(dev[:], st[:, :, 0], mean_ps[:, 0:NT], ALU.subtract).then_inc(small, 1)
                    dve.wait_ge(small, base + 1 + FREE)
                    nc.vector.tensor_tensor(nt1[:], dev[:], dev[:], ALU.mult).then_inc(small, 1)
                    dve.wait_ge(small, base + 2 + FREE)
                    nc.vector.tensor_tensor(tot[:], nt1[:], st[:, :, 1], ALU.add).then_inc(tot_ok, 1)
                    dve.wait_ge(var_ok, q + 1)
                    dve.wait_ge(sd_ok, q + 1)
                    nc.vector.tensor_scalar(var[:], var_ps[:, 0:NT], GN_EPS, -0.5, ALU.add, ALU.mult)
                    nc.vector.reciprocal(rs[:], sd[:]).then_inc(small, 1)
                    dve.wait_ge(small, base + 3 + FREE)
                    nc.vector.tensor_tensor(nt1[:], rs[:], rs[:], ALU.mult).then_inc(small, 1)
                    dve.wait_ge(small, base + 4 + FREE)
                    nc.vector.tensor_tensor(nt2[:], nt1[:], var[:], ALU.mult).then_inc(small, 1)
                    dve.wait_ge(small, base + 5 + FREE)
                    nc.vector.scalar_tensor_tensor(rstd[:], nt2[:], 1.5, rs[:], ALU.add, ALU.mult).then_inc(small, 1)
                    dve.wait_ge(small, base + 6 + FREE)
                    nc.vector.scalar_tensor_tensor(shift[:], mean_ps[:, 0:NT], -1.0, rstd[:], ALU.mult,
                                                   ALU.mult).then_inc(aff_ok, 1)
                    for c in range(NT):
                        dve.wait_ge(xhi_ok, q * NT + (c + 1))
                        nc.vector.tensor_tensor(xsplit[:, u, c, 1, :], xs[:, u, c, :], xsplit[:, u, c, 0, :],
                                                ALU.subtract).then_inc(xlo_ok, 1)


def main(nc, xt, cols_in, mask, sin_in, cos_in, ident_in, sign_in, out, w_scr, x_scr, wo_sb, fp32, fp16, ALU, ACT):
    with ExitStack() as ctx:
        def sb(name, shape, dt):
            return ctx.enter_context(nc.sbuf_tensor(name, shape, dt))

        def pb(name, shape, dt):
            return ctx.enter_context(nc.psum_tensor(name, shape, dt))

        def sem(name):
            return ctx.enter_context(nc.semaphore(name))

        cols = sb("cols", [P, NT, NCOL], fp32)
        pbias = sb("pbias", [P, NT, 3], fp32)
        biases = sb("biases", [P, 3], fp32)
        sin_sb = sb("sin_sb", [P, L], fp32)
        cos_sb = sb("cos_sb", [P, L], fp32)
        sign = sb("sign", [P, 1], fp32)
        ident = sb("ident", [P, P], fp32)
        xn = sb("xn", [P, NT, 2, L], fp16)
        w_sb = sb("w_sb", [P, 3, NT, 2, P], fp16)
        kq = sb("kq", [P, 2, L], fp32)
        kq_swap = sb("kq_swap", [P, 2, L], fp32)
        v_sb = sb("v_sb", [P, L], fp32)
        kq_hi = sb("kq_hi", [P, 2, L], fp16)
        kq_lo = sb("kq_lo", [P, 2, L], fp16)
        q_stack = sb("q_stack", [P, 2, L], fp16)
        k_hihi = sb("k_hihi", [P, 2, L], fp16)
        k_lolo = sb("k_lolo", [P, 2, L], fp16)
        v_nat = sb("v_nat", [P, NK, 2, 2, HD], fp16)
        mask_sb = sb("mask_sb", [P, 4, L], fp32)
        neg = sb("neg", [P, 2, L], fp32)
        neg_max = sb("neg_max", [P, NQ], fp32)
        rowsum = sb("rowsum", [P, NQ], fp32)
        rowrec = sb("rowrec", [P, NQ], fp32)
        prob = sb("prob", [P, 2, L], fp32)
        pt_hi = sb("pt_hi", [P, 2, L], fp16)
        pt_lo = sb("pt_lo", [P, 2, L], fp16)
        o_hi = sb("o_hi", [P, 2, 4, HD], fp32)
        o_sum = sb("o_sum", [P, 4, HD], fp32)
        o_nat = sb("o_nat", [P, NK, P], fp32)
        v_pad = sb("v_pad", [P, PSIDE, PSIDE], fp32)
        dw_cols = sb("dw_cols", [P, NCOL], fp32)
        dw = sb("dw", [P, L], fp32)
        tap = sb("tap", [P, 2, L], fp32)
        dw_all = sb("dw_all", [P, L], fp32)
        o_split = sb("o_split", [P, NT, 2, L], fp16)
        x_res = sb("x_res", [P, 2, HALF], fp32)
        out_sb = sb("out_sb", [P, 2, HALF], fp32)

        ps = pb("ps", [P, 2, 2, HALF], fp32)
        pt = pb("pt", [P, 2, HALF], fp32)
        pv = pb("pv", [P, 4, 2, HD], fp32)
        pj = pb("pj", [P, HALF], fp32)

        s_const = sem("s_const")
        s_ready = sem("s_ready")
        s_mask = [sem(f"s_mask{n}") for n in range(4)]
        s_wkq = sem("s_wkq")
        s_wv = sem("s_wv")
        s_xn = sem("s_xn")
        s_proj = sem("s_proj")
        s_pev = sem("s_pev")
        s_bias = sem("s_bias")
        s_swap = [sem(f"s_swap{n}") for n in range(2)]
        s_rot = sem("s_rot")
        s_rhi = sem("s_rhi")
        s_rlo = sem("s_rlo")
        s_rmul = sem("s_rmul")
        s_kstack = sem("s_kstack")
        s_qstack = sem("s_qstack")
        s_vt = sem("s_vt")
        s_vhi = sem("s_vhi")
        s_vlo = sem("s_vlo")
        s_vpad = sem("s_vpad")
        s_cols = sem("s_cols")
        s_s = sem("s_s")
        s_min = sem("s_min")
        s_exp = sem("s_exp")
        s_t = sem("s_t")
        s_hi = sem("s_hi")
        s_lo = sem("s_lo")
        s_pv = sem("s_pv")
        s_ohi = sem("s_ohi")
        s_rec = sem("s_rec")
        s_osum = sem("s_osum")
        s_on = sem("s_on")
        s_dw = sem("s_dw")
        s_mul = sem("s_mul")
        s_add = sem("s_add")
        s_ot = sem("s_ot")
        s_ota = sem("s_ota")
        s_othi = sem("s_othi")
        s_otlo = sem("s_otlo")
        s_op = sem("s_op")
        s_oev = sem("s_oev")
        s_xr = [sem(f"s_xr{n}") for n in range(2)]
        s_res = sem("s_res")
        s_store = [sem(f"s_store{n}") for n in range(2)]
        s_gate = [sem(f"s_gate{n}") for n in range(2)]
        s_stored = sem("s_stored")
        NCONST = 6

        block = ctx.enter_context(nc.Block())

        def steps(eng, step, after):
            with eng.Fori(0, B) as b:
                step(b * NT, b, 0, 1, True, False)
                with eng.Fori(1, NT - 1) as j:
                    step(b * NT + j, b, j, j + 1, False, False)
                step(b * NT + (NT - 1), b, NT - 1, 0, False, True)
                after(b)

        @block.sync
        def _(sp):
            sp.dma_start(cols[:], cols_in).then_inc(s_const, 16)
            sp.dma_start(w_sb[:, 0:2], w_scr[0, :, 0:2]).then_inc(s_wkq, 16)
            sp.dma_start(w_sb[:, 2], w_scr[0, :, 2]).then_inc(s_wv, 16)
            sp.dma_start(xn[:], x_scr[0]).then_inc(s_xn, 16)
            for dst, src in ((ident[:], ident_in), (sign[:], sign_in), (sin_sb[0:HD, :], sin_in), (sin_sb[HD:P, :], sin_in)):
                sp.dma_start(dst, src).then_inc(s_const, 16)
            for h in range(2):
                sp.dma_start(cos_sb[h * HD:(h + 1) * HD, :], cos_in).then_inc(s_const, 16)

            def swap(p, n):
                sp.wait_ge(s_pev, p * 6 + (2 * n + 2))
                for o in range(2):
                    sp.dma_start(kq_swap[o:P:2, n, :], kq[1 - o:P:2, n, :]).then_inc(s_swap[n], 16)

            def stack_k(p, h):
                sp.wait_ge(s_rlo, p * 2 + 1)
                for r in range(2):
                    for dst, src in ((k_hihi, kq_hi), (k_lolo, kq_lo)):
                        sp.dma_start(dst[r * HD:(r + 1) * HD, h, :],
                                     src[h * HD:(h + 1) * HD, 0, :]).then_inc(s_kstack, 16)

            def stack_q(p):
                sp.wait_ge(s_rlo, p * 2 + 2)
                for h in range(2):
                    for r, src in enumerate((kq_hi, kq_lo)):
                        sp.dma_start(q_stack[r * HD:(r + 1) * HD, h, :],
                                     src[h * HD:(h + 1) * HD, 1, :]).then_inc(s_qstack, 16)

            def weights_kq(p, j):
                sp.wait_ge(s_proj, p * 6 + 4)
                sp.dma_start(w_sb[:, 0:2], w_scr[j, :, 0:2]).then_inc(s_wkq, 16)

            for n in range(2):
                swap(0, n)
            weights_kq(0, 1)
            for h in range(2):
                stack_k(0, h)
            stack_q(0)

            def step(t, b, j, jn, first, last):
                late = LATE if last else 0
                for i in range(NQ):
                    sp.wait_ge(s_min, t * NQ + max(i - 3, 0) + FREE)
                    sp.dma_start(mask_sb[:, i % 4, :], mask[j * 2 + i // NK, i % NK]).then_inc(s_mask[i % 4], 16)
                    if i == 3:
                        sp.wait_ge(s_proj, t * 6 + 6)
                        if last:
                            sp.dma_start(xn[:], x_scr[b + 1]).then_inc(s_xn, 16)
                        sp.dma_start(w_sb[:, 2], w_scr[jn, :, 2]).then_inc(s_wv, 16)
                    if i == 8 + late:
                        swap(t + 1, 0)
                    if i == 13 and not last:
                        stack_k(t + 1, 0)
                swap(t + 1, 1)
                weights_kq(t + 1, j + 2)
                sp.wait_ge(s_s, t * NQ + NQ)
                if last:
                    stack_k(t + 1, 0)
                stack_k(t + 1, 1)
                stack_q(t + 1)

            steps(sp, step, lambda b: None)
            sp.wait_ge(s_kstack, 128 * (B * NT + 1))
            sp.wait_ge(s_qstack, 64 * (B * NT + 1))
            sp.wait_ge(s_wkq, 16 * (B * NT + 2))

        @block.gpsimd
        def _(pool):
            def step(t, b, j, jn, first, last):
                for k in range(1, POOL_TAPS + 1):
                    if k < POOL_TAPS:
                        pool.wait_ge(s_mul, t * POOL_TAPS + (k + 1))
                    else:
                        pool.wait_ge(s_dw, t * DVE_TAPS + DVE_TAPS)
                    if k == 1:
                        pool.wait_ge(s_otlo, t + FREE)
                    else:
                        pool.wait_ge(s_add, t * POOL_TAPS + (k - 1) + FREE)
                    nc.gpsimd.tensor_tensor(dw_all[:], tap[:, 0] if k == 1 else dw_all[:],
                                            tap[:, k % 2] if k < POOL_TAPS else dw[:], ALU.add).then_inc(s_add, 1)

            def after(b):
                def load(a):
                    pool.dma_start(x_res[:, a % 2, :],
                                   xt[b, :, a // 2, a % 2 * HALF:(a % 2 + 1) * HALF]).then_inc(s_xr[a % 2], 16)

                pool.wait_ge(s_res, b * 2 * NT + FREE)
                pool.sem_inc(s_gate[1], 1)
                load(0)
                load(1)
                for a in range(2 * NT):
                    pool.wait_ge(s_res, b * 2 * NT + (a + 1) + FREE)
                    pool.sem_inc(s_gate[1], 1)
                    pool.dma_start(out[b, :, a // 2, a % 2 * HALF:(a % 2 + 1) * HALF],
                                   out_sb[:, a % 2, :]).then_inc(s_store[a % 2], 16)
                    if a + 2 < 2 * NT:
                        load(a + 2)
                    if a > 0:
                        pool.wait_ge(s_store[(a - 1) % 2], b * 16 * NT + 16 * ((a - 1) // 2 + 1))
                        pool.sem_inc(s_stored, 1)
                pool.wait_ge(s_store[1], b * 16 * NT + 16 * NT)
                pool.sem_inc(s_stored, 1)

            steps(pool, step, after)

        @block.scalar
        def _(act):
            act.wait_ge(s_ready, 4)

            def own_biases(p, jn):
                nc.scalar.activation(biases[:], pbias[:, jn, :], ACT.Copy).then_inc(s_bias, 1)
                act.wait_ge(s_bias, p + 1)

            def copy_out(p, a):
                act.wait_ge(s_proj, p * 6 + (a + 1))
                n, half = a // 2, slice(a % 2 * HALF, (a % 2 + 1) * HALF)
                nc.scalar.activation(v_sb[:, half] if n == 2 else kq[:, n, half], pj[:],
                                     ACT.Identity, bias=biases[:, n:n + 1],
                                     scale=(HD ** -0.5 if n == 0 else 1.0) / W_SCALE).then_inc(s_pev, 1)

            def rotated_high(p, n):
                act.wait_ge(s_rot, p * 2 + (n + 1))
                nc.scalar.activation(kq_hi[:, n, :], kq[:, n, :], ACT.Copy).then_inc(s_rhi, 1)

            def value_highs(p):
                for h in range(2):
                    act.wait_ge(s_vt, p * 2 + (h + 1))
                    nc.scalar.activation(v_nat[:, 4 * h:4 * h + 4, :, 0, :],
                                         ps[:, 1, h, :].rearrange("p (k h c) -> p k h c", k=4, h=2),
                                         ACT.Copy).then_inc(s_vhi, 1)

            def pad(n):
                nc.scalar.activation(v_pad[:, PAD:PAD + SIDE, PAD:PAD + SIDE],
                                     v_sb[:].rearrange("p (r c) -> p r c", c=SIDE), ACT.Copy).then_inc(s_vpad, 1)

            own_biases(0, 0)
            for a in range(4):
                copy_out(0, a)
            rotated_high(0, 0)
            copy_out(0, 4)
            copy_out(0, 5)
            rotated_high(0, 1)
            value_highs(0)
            act.wait_ge(s_pev, 6)
            pad(0)

            def step(t, b, j, jn, first, last):
                def high(i):
                    for h in range(2):
                        act.wait_ge(s_t, t * 2 * NQ + (2 * i + h + 1) + FREE)
                        if h == 0:
                            act.wait_ge(s_pv, t * NQ + max(i - 1, 0) + FREE)
                        nc.scalar.activation(pt_hi[:, i % 2, h * HALF:(h + 1) * HALF], pt[:, h, :], ACT.Copy,
                                             scale=P_SCALE).then_inc(s_hi, 1)

                def group(g):
                    act.wait_ge(s_pv, t * NQ + 4 * (g + 1) + FREE)
                    nc.scalar.activation(o_hi[:, g % 2], pv[:, :, 0, :], ACT.Copy,
                                         scale=1.0 / P_SCALE).then_inc(s_ohi, 1)

                def tap_products(k):
                    r, c = k // KS, k % KS
                    if k == 0:
                        act.wait_ge(s_cols, t + 1)
                        act.wait_ge(s_vpad, t + 1)
                    act.wait_ge(s_add, t * POOL_TAPS + (max(k - 2, 1) if k > 1 else 0) + FREE)
                    nc.scalar.activation(tap[:, k % 2].rearrange("p (r c) -> p r c", c=SIDE),
                                         v_pad[:, r:r + SIDE, c:c + SIDE], ACT.Identity, scale=dw_cols[:, k:k + 1],
                                         bias=dw_cols[:, COL_LB:COL_LB + 1] if k == 0 else 0.0).then_inc(s_mul, 1)

                def output_high(p, k):
                    act.wait_ge(s_ota, p * 2 + 2 + FREE)
                    nc.scalar.activation(o_split[:, k, 0, :], dw_all[:], ACT.Copy).then_inc(s_othi, 1)

                late = LATE if last else 0
                own_biases(t + 1, jn)
                for i in range(NQ + 5):
                    if i >= LAG + 5 and (i - LAG - 5) % 4 == 0:
                        group((i - LAG - 5) // 4)
                    for a in range(6):
                        if i == 3 * a + 3 + late and not (last and a > 3):
                            copy_out(t + 1, a)
                    for n in range(2):
                        if i == 9 + 6 * n + late:
                            rotated_high(t + 1, n)
                    if i == 2 and not first:
                        output_high(t - 1, j - 1)
                    if LAG <= i < NQ + LAG:
                        high(i - LAG)
                    if i < NQ:
                        act.wait_ge(s_min, t * NQ + (i + 1) + FREE)
                        act.wait_ge(s_t, t * 2 * NQ + max(2 * (i - 1), 0) + FREE)
                        nc.scalar.activation(prob[:, i % 2, :], neg[:, i % 2, :], ACT.Exp, scale=-1.0,
                                             bias=neg_max[:, i:i + 1], accum_out=rowsum[:, i:i + 1]).then_inc(s_exp, 1)
                    if i < 2:
                        tap_products(i)
                    elif 3 <= i <= POOL_TAPS:
                        tap_products(i - 1)
                if last:
                    copy_out(t + 1, 4)
                    output_high(t, j)
                    copy_out(t + 1, 5)
                value_highs(t + 1)
                act.wait_ge(s_dw, t * DVE_TAPS + DVE_TAPS)
                pad(t)

            def after(b):
                for a in range(2 * NT):
                    m, h = a // 2, a % 2
                    act.wait_ge(s_op, b * 2 * NT + (a + 1))
                    act.wait_ge(s_stored, b * 2 * NT + max(a - 1, 0) + FREE)
                    nc.scalar.activation(out_sb[:, a % 2, :], ps[:, (a // 2) % 2, h, :],
                                         ACT.Identity, bias=cols[:, m, COL_O:COL_O + 1],
                                         scale=1.0 / W_SCALE).then_inc(s_oev, 1)

            steps(act, step, after)

        @block.tensor
        def _(pe):
            TERMS = ((0, 0), (0, 1), (1, 0))
            PER = NT * len(TERMS)

            def project(p, start, stop):
                for x in range(start, stop):
                    a, y = x // PER, x % PER
                    n, h, k = a // 2, a % 2, y // len(TERMS)
                    s, m = TERMS[y % len(TERMS)]
                    if y == 0 and a > 0:
                        pe.wait_ge(s_pev, p * 6 + a)
                    mm = nc.tensor.matmul(pj[:], w_sb[:, n, k, s, :],
                                          xn[:, k, m, h * HALF:(h + 1) * HALF], start=(y == 0), stop=(y == PER - 1))
                    if y == PER - 1:
                        mm.then_inc(s_proj, 1)

            def turn_values(p, first):
                for h in range(2):
                    pe.wait_ge(s_pev, p * 6 + (5 + h))
                    if not first:
                        pe.wait_ge(s_min, p * NQ + FREE)
                    for k in range(4):
                        mm = nc.tensor.transpose(ps[:, 1, h, k * P:(k + 1) * P],
                                                 v_sb[:, h * HALF + k * P:h * HALF + (k + 1) * P], ident[:])
                    mm.then_inc(s_vt, 1)

            pe.wait_ge(s_const, 16 * (NCONST + 1))
            pe.wait_ge(s_wkq, 16)
            pe.wait_ge(s_wv, 16)
            pe.wait_ge(s_xn, 16)
            project(0, 0, 6 * PER)
            turn_values(0, True)

            def step(t, b, j, jn, first, last):
                def scores(i):
                    h, q = i // NK, i % NK
                    if i == 0:
                        pe.wait_ge(s_kstack, t * 128 + 128)
                        pe.wait_ge(s_qstack, t * 64 + 64)
                        pe.wait_ge(s_oev, b * 2 * NT + FREE)
                    if i == 1:
                        pe.wait_ge(s_vlo, t * 2 + 2)
                    if i >= 2:
                        pe.wait_ge(s_min, t * NQ + (i - 1) + FREE)
                    for s, k_part in enumerate((k_hihi, k_lolo)):
                        for n in range(2):
                            mm = nc.tensor.matmul(ps[:, i % 2, n, :], q_stack[:, h, q * P:(q + 1) * P],
                                                  k_part[:, h, n * HALF:(n + 1) * HALF], start=(s == 0), stop=(s == 1))
                    mm.then_inc(s_s, 1)

                def transposes(i):
                    pe.wait_ge(s_exp, t * NQ + (i + 1) + FREE)
                    for h in range(2):
                        if i == 0:
                            pe.wait_ge(s_ota, t * 2 + FREE)
                        else:
                            pe.wait_ge(s_lo, t * 2 * NQ + (2 * i - 1 + h))
                        for k in range(4):
                            c = (4 * h + k) * P
                            mm = nc.tensor.transpose(pt[:, h, k * P:(k + 1) * P], prob[:, i % 2, c:c + P], ident[:])
                        mm.then_inc(s_t, 1)

                def values(i):
                    h, g = i // NK, i // 4
                    if i % 4 == 0:
                        pe.wait_ge(s_osum, t * 4 + g + FREE)
                    pe.wait_ge(s_lo, t * 2 * NQ + (2 * i + 2))
                    for s, part in enumerate((pt_hi, pt_lo)):
                        for k in range(NK):
                            mm = nc.tensor.matmul(pv[:, i % 4].rearrange("p a c -> p (a c)"),
                                                  part[:, i % 2, k * P:(k + 1) * P],
                                                  v_nat[:, k, h].rearrange("p a c -> p (a c)"),
                                                  start=(s == 0 and k == 0), stop=(s == 1 and k == NK - 1))
                    mm.then_inc(s_pv, 1)

                def turn_outputs(p):
                    pe.wait_ge(s_on, p * 4 + 4)
                    pe.wait_ge(s_lo, p * 2 * NQ + 2 * NQ)
                    for h in range(2):
                        for k in range(4):
                            mm = nc.tensor.transpose(pt[:, h, k * P:(k + 1) * P], o_nat[:, 4 * h + k, :], ident[:])
                        mm.then_inc(s_ot, 1)

                late = LATE if last else 0
                for i in range(NQ + LAG + 1):
                    if i < NQ:
                        scores(i)
                    if i == 1 and not first:
                        turn_outputs(t - 1)
                    if LAG <= i < NQ + LAG:
                        transposes(i - LAG)
                    if i == late:
                        pe.wait_ge(s_wkq, t * 16 + 32)
                        pe.wait_ge(s_pev, t * 6 + 6)
                        if last:
                            pe.wait_ge(s_xn, b * 16 + 32)
                    if i == 12 and not last:
                        pe.wait_ge(s_wv, t * 16 + 32)
                    start = (i - late) * PER // 3
                    here = late <= i < (NQ if last else NQ + LAG)
                    if LAG < i and start % PER == 0:
                        values(i - LAG - 1)
                    if here:
                        project(t + 1, start, start + PER // 3)
                    if LAG < i and start % PER != 0:
                        values(i - LAG - 1)
                if last:
                    pe.wait_ge(s_wv, t * 16 + 32)
                    project(t + 1, 4 * PER, 5 * PER)
                    turn_outputs(t)
                    project(t + 1, 5 * PER, 6 * PER)
                turn_values(t + 1, False)

            def after(b):
                pe.wait_ge(s_otlo, b * NT + NT + FREE)
                pe.wait_ge(s_pev, b * 6 * NT + 6 * (NT + 1))
                for a in range(2 * NT):
                    m, h = a // 2, a % 2
                    if a == 2:
                        pe.wait_ge(s_vlo, b * 2 * NT + 2 * (NT + 1))
                    if a >= 4:
                        pe.wait_ge(s_oev, b * 2 * NT + (a - 3) + FREE)
                    for k in range(NT):
                        for s, r in TERMS:
                            mm = nc.tensor.matmul(ps[:, m % 2, h, :], wo_sb[:, k, s, m * P:(m + 1) * P],
                                                  o_split[:, k, r, h * HALF:(h + 1) * HALF],
                                                  start=(k == 0 and (s, r) == TERMS[0]),
                                                  stop=(k == NT - 1 and (s, r) == TERMS[-1]))
                    mm.then_inc(s_op, 1)

            steps(pe, step, after)

        @block.vector
        def _(dve):
            for free in (s_min, s_res, s_pv, s_t, s_oev, s_ota, s_osum, s_exp, s_othi, s_otlo, s_stored, s_add):
                dve.sem_inc(free, FREE)
            nc.vector.memset(v_pad[:], 0.0).then_inc(s_ready, 1)
            dve.wait_ge(s_const, 16 * (NCONST + 1))
            nc.vector.tensor_scalar(pbias[:, :, 0], cols[:, :, COL_K], HD ** -0.5, None, ALU.mult).then_inc(s_ready, 1)
            nc.vector.tensor_copy(pbias[:, :, 1:3], cols[:, :, COL_Q:COL_V + 1]).then_inc(s_ready, 1)
            nc.vector.tensor_scalar(sin_sb[:], sin_sb[:], sign[:, 0:1], None, ALU.mult).then_inc(s_ready, 1)
            dve.wait_ge(s_ready, 4)

            def rotate_products(p, n):
                dve.wait_ge(s_swap[n], p * 32 + 32)
                nc.vector.tensor_tensor(kq[:, n, :], kq[:, n, :], cos_sb[:], ALU.mult).then_inc(s_rmul, 1)
                nc.vector.tensor_tensor(kq_swap[:, n, :], kq_swap[:, n, :], sin_sb[:], ALU.mult).then_inc(s_rmul, 1)

            def rotate_sum(p, n):
                dve.wait_ge(s_rmul, p * 4 + 2 * (n + 1))
                nc.vector.tensor_tensor(kq[:, n, :], kq[:, n, :], kq_swap[:, n, :], ALU.add).then_inc(s_rot, 1)

            def rotated_low(p, n):
                dve.wait_ge(s_rhi, p * 2 + (n + 1))
                nc.vector.tensor_tensor(kq_lo[:, n, :], kq[:, n, :], kq_hi[:, n, :], ALU.subtract).then_inc(s_rlo, 1)

            def value_lows(p):
                for h in range(2):
                    dve.wait_ge(s_vhi, p * 2 + (h + 1))
                    nc.vector.tensor_tensor(v_nat[:, 4 * h:4 * h + 4, :, 1, :],
                                            ps[:, 1, h, :].rearrange("p (k h c) -> p k h c", k=4, h=2),
                                            v_nat[:, 4 * h:4 * h + 4, :, 0, :], ALU.subtract).then_inc(s_vlo, 1)

            for n in range(2):
                rotate_products(0, n)
                rotate_sum(0, n)
                rotated_low(0, n)
            value_lows(0)

            def step(t, b, j, jn, first, last):
                done = [0]

                image = dw[:].rearrange("p (r c) -> p r c", c=SIDE)

                def taps(n):
                    for _ in range(n):
                        k = done[0]
                        if k >= DVE_TAPS:
                            return
                        w = POOL_TAPS + k
                        r, c = w // KS, w % KS
                        src = v_pad[:, r:r + SIDE, c:c + SIDE]
                        if k == 0:
                            dve.wait_ge(s_vpad, t + 1)
                            dve.wait_ge(s_cols, t + 1)
                            dve.wait_ge(s_add, t * POOL_TAPS + FREE)
                            ins = nc.vector.tensor_scalar(image, src, dw_cols[:, w:w + 1], None, ALU.mult)
                        else:
                            dve.wait_ge(s_dw, t * DVE_TAPS + k)
                            ins = nc.vector.scalar_tensor_tensor(image, src, dw_cols[:, w:w + 1], image,
                                                                 ALU.mult, ALU.add)
                        ins.then_inc(s_dw, 1)
                        done[0] += 1

                def low(i):
                    for h in range(2):
                        dve.wait_ge(s_hi, t * 2 * NQ + (2 * i + h + 1))
                        nc.vector.scalar_tensor_tensor(pt_lo[:, i % 2, h * HALF:(h + 1) * HALF], pt[:, h, :], P_SCALE,
                                                       pt_hi[:, i % 2, h * HALF:(h + 1) * HALF],
                                                       ALU.mult, ALU.subtract).then_inc(s_lo, 1)

                def group(g):
                    h = g // 2
                    dve.wait_ge(s_ohi, t * 4 + (g + 1))
                    nc.vector.reciprocal(rowrec[:, 4 * g:4 * g + 4], rowsum[:, 4 * g:4 * g + 4]).then_inc(s_rec, 1)
                    nc.vector.scalar_tensor_tensor(o_sum[:], pv[:, :, 1, :], 1.0 / P_SCALE, o_hi[:, g % 2],
                                                   ALU.mult, ALU.add).then_inc(s_osum, 1)
                    dve.wait_ge(s_rec, t * 4 + (g + 1))
                    dve.wait_ge(s_osum, t * 4 + (g + 1) + FREE)
                    nc.vector.tensor_tensor(o_nat[:, 4 * (g % 2):4 * (g % 2) + 4, h * HD:(h + 1) * HD], o_sum[:],
                                            rowrec[:, 4 * g:4 * g + 4].unsqueeze(2).to_broadcast([P, 4, HD]),
                                            ALU.mult).then_inc(s_on, 1)

                def output_sum(p):
                    for h in range(2):
                        dve.wait_ge(s_ot, p * 2 + (h + 1))
                        if h == 0:
                            dve.wait_ge(s_add, (p + 1) * POOL_TAPS + FREE)
                        nc.vector.tensor_tensor(dw_all[:, h * HALF:(h + 1) * HALF], pt[:, h, :],
                                                dw_all[:, h * HALF:(h + 1) * HALF], ALU.add).then_inc(s_ota, 1)

                def output_low(p, k):
                    dve.wait_ge(s_othi, p + 1 + FREE)
                    nc.vector.tensor_tensor(o_split[:, k, 1, :], dw_all[:], o_split[:, k, 0, :],
                                            ALU.subtract).then_inc(s_otlo, 1)

                late = LATE if last else 0
                nc.vector.tensor_copy(dw_cols[:], cols[:, j, :]).then_inc(s_cols, 1)
                for i in range(NQ + 5):
                    if i >= LAG + 5 and (i - LAG - 5) % 4 == 0:
                        group((i - LAG - 5) // 4)
                    if i < NQ:
                        dve.wait_ge(s_s, t * NQ + (i + 1))
                        dve.wait_ge(s_exp, t * NQ + max(i - 1, 0) + FREE)
                        dve.wait_ge(s_mask[i % 4], t * 64 + 16 * (i // 4 + 1))
                        dve.sem_inc(s_gate[0], 1)
                        nc.vector.tensor_tensor_reduce(out=neg[:, i % 2, :], in0=ps[:, i % 2].rearrange("p a n -> p (a n)"),
                                                       in1=mask_sb[:, i % 4, :], scale=-1.0, scalar=BIG, op0=ALU.add,
                                                       op1=ALU.min, accum_out=neg_max[:, i:i + 1]).then_inc(s_min, 1)
                    if LAG <= i < NQ + LAG:
                        low(i - LAG)
                    if i == 1 and not first:
                        output_sum(t - 1)
                    if i == 2 and not first:
                        output_low(t - 1, j - 1)
                    taps({0: 2, 1: 1, 3: 1, 4: 2, 5: 1, 6: 1, 9: 1, 11: 1, 12: 1}.get(i, 0))
                    for n in range(2):
                        if i == 7 + 6 * n + late:
                            rotate_products(t + 1, n)
                        if i == 8 + 6 * n + late:
                            rotate_sum(t + 1, n)
                        if i == 10 + 6 * n + late:
                            rotated_low(t + 1, n)
                if last:
                    output_sum(t)
                    output_low(t, j)
                value_lows(t + 1)

            def after(b):
                for a in range(2 * NT):
                    m, h = a // 2, a % 2
                    dve.wait_ge(s_oev, b * 2 * NT + (a + 1) + FREE)
                    dve.wait_ge(s_xr[a % 2], b * 16 * NT + 16 * (a // 2 + 1))
                    nc.vector.tensor_tensor(out_sb[:, a % 2, :], out_sb[:, a % 2, :], x_res[:, a % 2, :],
                                            ALU.add).then_inc(s_res, 1)

            steps(dve, step, after)


def kernel(**inputs):
    import numpy as np
    import concourse.bacc as bacc
    from concourse.bass_utils import run_bass_kernel_spmd

    a = {k.removeprefix("L0_conv_"): np.asarray(v) for k, v in inputs.items()}
    tiles = lambda w: w.reshape(NT, P, NT, P).transpose(0, 3, 2, 1)
    lanes = lambda v: v.reshape(NT, P).T
    f = np.float32
    arrays = {
        "xt": a["x"].reshape(B, L, NT, P).transpose(0, 3, 2, 1),
        "w3": np.stack([tiles(a["wk"]), tiles(a["wq"]), tiles(a["wv"])], axis=2).reshape(NT, P, 3 * NT * P),
        "wo": a["wo"].T.reshape(NT, P, C).transpose(1, 0, 2),
        "cols": np.stack([lanes(t) for t in a["lepe_w"].reshape(TAPS, C)]
                         + [lanes(a[n]) for n in ("lepe_b", "bk", "bq", "bv", "bo")], axis=2),
        "mask": a["mask"].reshape(NH, NK, P, L),
        "sin": a["sin"].reshape(L, HD).T,
        "cos": a["cos"].reshape(L, HD).T,
        "ident": np.eye(P, dtype=f),
        "gavg": (np.equal.outer(np.arange(C) // (C // GROUPS), np.arange(C) // (C // GROUPS)).astype(f)
                 * f(GROUPS / C)).reshape(NT, P, C).transpose(1, 0, 2),
        "sign": np.where(np.arange(P) % 2 == 0, -1, 1).astype(f).reshape(P, 1),
    }
    arrays = {k: np.ascontiguousarray(v) for k, v in arrays.items()}
    nc = bacc.Bacc("TRN2", target_bir_lowering=False, num_devices=1)
    fp32, fp16 = mybir.dt.float32, mybir.dt.float16
    d = {k: nc.dram_tensor(f"{k}_in", v.shape, fp32, kind="ExternalInput").ap() for k, v in arrays.items()}
    out = nc.dram_tensor("out_t", (B, P, NT, L), fp32, kind="ExternalOutput").ap()
    w_scr = nc.dram_tensor("w_scr", (NT + 2, P, 3, NT, 2, P), fp16, kind="Internal").ap()
    x_scr = nc.dram_tensor("x_scr", (B + 1, P, NT, 2, L), fp16, kind="Internal").ap()
    conv_preact(nc, d["xt"], d["w3"], d["wo"], d["cols"], d["mask"], d["sin"], d["cos"], d["ident"], d["gavg"],
                d["sign"], out, w_scr, x_scr)
    r = run_bass_kernel_spmd(nc, [{f"{k}_in": v for k, v in arrays.items()}], core_ids=[0])
    got = r.results[0]["out_t"]
    return np.ascontiguousarray(got.transpose(0, 3, 2, 1)).reshape(B, SIDE, SIDE, C)
```

```python
import concourse.bass as bass
from concourse import mybir
from contextlib import ExitStack

FP32, FP16 = mybir.dt.float32, mybir.dt.float16
ALU, ACT = mybir.AluOpType, mybir.ActivationFunctionType

B, SIDE, C, NH = 8, 32, 768, 12
L = SIDE * SIDE
HD = C // NH
P = 128
NT = C // P
HALF = 512
NK = L // P
NQ = 2 * NK
KS = 5
PAD = KS // 2
PSIDE = SIDE + 2 * PAD
TAPS = KS * KS
POOL_TAPS = 14
DVE_TAPS = TAPS - POOL_TAPS
DW_AT = POOL_TAPS - 2
LAG = 2
LATE = 7
GROUPS = 32
W_SCALE = 256.0
P_SCALE = 4096.0
GN_EPS = 1e-5
BIG = 3.0e38
FREE = 1
COL_LB, COL_K, COL_Q, COL_V, COL_O, NCOL = TAPS, TAPS + 1, TAPS + 2, TAPS + 3, TAPS + 4, TAPS + 5


def conv_preact(nc, xt, w3, wo, cols_in, mask, sin_in, cos_in, ident_in, gavg_in, sign_in, out, w_scr):
    with ExitStack() as top:
        g = Shared(nc, top)
        prepare(nc, g, xt, w3, wo, cols_in, sin_in, cos_in, ident_in, gavg_in, sign_in, w_scr)
        main(nc, g, xt, mask, gavg_in, out, w_scr)


class Shared:
    SMALL = NT - 1 + 6

    def __init__(self, nc, ctx):
        def sb(name, shape, dt):
            return ctx.enter_context(nc.sbuf_tensor(name, shape, dt))

        def sem(name):
            return ctx.enter_context(nc.semaphore(name))

        self.nc = nc
        self.wo_sb = sb("wo_sb", [P, NT, 2, C], FP16)
        self.cols = sb("cols", [P, NT, NCOL], FP32)
        self.sin_sb = sb("sin_sb", [P, L], FP32)
        self.cos_sb = sb("cos_sb", [P, L], FP32)
        self.sign = sb("sign", [P, 1], FP32)
        self.ident = sb("ident", [P, P], FP32)
        self.eps = sb("eps", [P, 1], FP32)
        self.xraw = sb("xraw", [P, NT, L], FP32)
        self.xn = self.xraw[:].bitcast(FP16).rearrange("p c (r l) -> p c r l", r=2)
        self.kq = sb("kq", [P, 2, L], FP32)
        self.kq_swap = sb("kq_swap", [P, 2, L], FP32)
        self.v_sb = sb("v_sb", [P, L], FP32)
        self.gavg = self.kq[:].rearrange("p a l -> p (a l)")[:, 0:3 * 3 * P].rearrange("p (k o) -> p k o", k=3)
        self.tmp = [self.kq_swap[:, 0, :], self.kq_swap[:, 1, :], self.v_sb[:]]
        self.bn = sb("bn", [P, NT, 2, 6], FP32)
        self.st = sb("st", [P, NT, 2], FP32)
        self.dev = sb("dev", [P, NT], FP32)
        self.tot = sb("tot", [P, NT], FP32)
        self.var = sb("var", [P, NT], FP32)
        self.sd = sb("sd", [P, NT], FP32)
        self.rs = sb("rs", [P, NT], FP32)
        self.nt1 = sb("nt1", [P, NT], FP32)
        self.nt2 = sb("nt2", [P, NT], FP32)
        self.rstd = sb("rstd", [P, NT], FP32)
        self.shift = sb("shift", [P, NT], FP32)
        self.pj = ctx.enter_context(nc.psum_tensor("pj", [P, HALF], FP32))
        self.mean_ps = self.pj[:, 0:NT]
        self.var_ps = self.pj[:, NT:2 * NT]

        self.s_const = sem("s_const")
        self.gavg_ok = sem("gavg_ok")
        self.x_in = [sem(f"x_in{n}") for n in range(2)]
        self.bn_ok = sem("bn_ok")
        self.st_ok = sem("st_ok")
        self.mean_ok = sem("mean_ok")
        self.tot_ok = sem("tot_ok")
        self.var_ok = sem("var_ok")
        self.sd_ok = sem("sd_ok")
        self.small = sem("small")
        self.aff_ok = sem("aff_ok")
        self.xaff_ok = sem("xaff_ok")
        self.xhi_ok = sem("xhi_ok")
        self.xlo_ok = sem("xlo_ok")
        self.gate = sem("gate")

    def load_gavg(self, sp, gavg_in):
        sp.dma_start(self.gavg, gavg_in).then_inc(self.gavg_ok, 16)

    def load(self, sp, xt, q, n):
        sp.dma_start(self.xraw[:, 3 * n:3 * n + 3, :], xt[q, :, 3 * n:3 * n + 3, :]).then_inc(self.x_in[n], 16)

    def stats(self, dve, c, src):
        for h in range(2):
            self.nc.vector.bn_stats(self.bn[:, c, h, :], src[:, h * HALF:(h + 1) * HALF]).then_inc(self.bn_ok, 1)

    def aggregate(self, dve, q):
        dve.wait_ge(self.bn_ok, q * 2 * NT + 2 * NT)
        dve.sem_inc(self.gate, 1)
        for c in range(NT):
            last = self.nc.vector.bn_aggr(self.st[:, c, :], self.bn[:, c, :, :])
            if c < NT - 1:
                last.then_inc(self.small, 1)
        last.then_inc(self.st_ok, 1)

    def average(self, pe, q, what):
        dst, src, ready, done = ((self.mean_ps, self.st[:, :, 0], self.st_ok, self.mean_ok),
                                 (self.var_ps, self.tot[:], self.tot_ok, self.var_ok))[what]
        if what == 0:
            pe.wait_ge(self.gavg_ok, q * 16 + 16)
        pe.wait_ge(ready, q + 1)
        for m in range(3):
            for k in range(3):
                last = self.nc.tensor.matmul(dst[:, m:NT:3], self.gavg[:, k, m * P:(m + 1) * P],
                                             src[:, k:NT:3], start=(k == 0), stop=(k == 2))
        last.then_inc(done, 1)

    def deviations(self, dve, q):
        nc, base = self.nc, q * self.SMALL + (NT - 1)
        dve.wait_ge(self.mean_ok, q + 1)
        nc.vector.tensor_tensor(self.dev[:], self.st[:, :, 0], self.mean_ps, ALU.subtract).then_inc(self.small, 1)
        dve.wait_ge(self.small, base + 1 + FREE)
        nc.vector.tensor_tensor(self.nt1[:], self.dev[:], self.dev[:], ALU.mult).then_inc(self.small, 1)
        dve.wait_ge(self.small, base + 2 + FREE)
        nc.vector.tensor_tensor(self.tot[:], self.nt1[:], self.st[:, :, 1], ALU.add).then_inc(self.tot_ok, 1)

    def root(self, act, q):
        act.wait_ge(self.var_ok, q + 1)
        self.nc.scalar.activation(self.sd[:], self.var_ps, ACT.Sqrt, bias=self.eps[:, 0:1]).then_inc(self.sd_ok, 1)

    def scale_shift(self, dve, q):
        nc, base = self.nc, q * self.SMALL + (NT - 1)
        dve.wait_ge(self.var_ok, q + 1)
        dve.wait_ge(self.sd_ok, q + 1)
        nc.vector.tensor_scalar(self.var[:], self.var_ps, GN_EPS, -0.5, ALU.add, ALU.mult)
        nc.vector.reciprocal(self.rs[:], self.sd[:]).then_inc(self.small, 1)
        dve.wait_ge(self.small, base + 3 + FREE)
        nc.vector.tensor_tensor(self.nt1[:], self.rs[:], self.rs[:], ALU.mult).then_inc(self.small, 1)
        dve.wait_ge(self.small, base + 4 + FREE)
        nc.vector.tensor_tensor(self.nt2[:], self.nt1[:], self.var[:], ALU.mult).then_inc(self.small, 1)
        dve.wait_ge(self.small, base + 5 + FREE)
        nc.vector.scalar_tensor_tensor(self.rstd[:], self.nt2[:], 1.5, self.rs[:], ALU.add, ALU.mult).then_inc(self.small, 1)
        dve.wait_ge(self.small, base + 6 + FREE)
        nc.vector.scalar_tensor_tensor(self.shift[:], self.mean_ps, -1.0, self.rstd[:], ALU.mult,
                                       ALU.mult).then_inc(self.aff_ok, 1)

    def apply(self, pool, q, c):
        if c == 0:
            pool.wait_ge(self.aff_ok, q + 1)
        if c % 3 == 0:
            pool.wait_ge(self.x_in[c // 3], q * 16 + 16)
        if c >= 3:
            pool.wait_ge(self.xlo_ok, q * NT + (c - 2))
        if c == 0 or c >= 3:
            pool.sem_inc(self.gate, 1)
        self.nc.gpsimd.tensor_scalar(self.tmp[c % 3], self.xraw[:, c, :], self.rstd[:, c:c + 1],
                                     self.shift[:, c:c + 1], ALU.mult, ALU.add).then_inc(self.xaff_ok, 1)

    def high(self, act, q, c):
        act.wait_ge(self.xaff_ok, q * NT + (c + 1))
        self.nc.scalar.activation(self.xn[:, c, 0, :], self.tmp[c % 3], ACT.Copy).then_inc(self.xhi_ok, 1)

    def low(self, dve, q, c):
        dve.wait_ge(self.xhi_ok, q * NT + (c + 1))
        self.nc.vector.tensor_tensor(self.xn[:, c, 1, :], self.tmp[c % 3], self.xn[:, c, 0, :],
                                     ALU.subtract).then_inc(self.xlo_ok, 1)


def prepare(nc, g, xt, w3, wo, cols_in, sin_in, cos_in, ident_in, gavg_in, sign_in, w_scr):
    with ExitStack() as ctx:
        def sb(name, shape, dt):
            return ctx.enter_context(nc.sbuf_tensor(name, shape, dt))

        def sem(name):
            return ctx.enter_context(nc.semaphore(name))

        wraw = sb("wraw", [P, NT, 3 * NT * P], FP32)
        wsplit = sb("wsplit", [P, NT, 3 * NT, 2, P], FP16)
        woraw = sb("woraw", [P, NT, C], FP32)

        w_in = [sem(f"w_in{n}") for n in range(NT)]
        w_out = sem("w_out")
        wo_in = sem("wo_in")
        w_hi = sem("w_hi")
        w_lo = sem("w_lo")
        eps_ok = sem("eps_ok")

        block = ctx.enter_context(nc.Block())

        @block.sync
        def _(sp):
            g.load(sp, xt, 0, 0)
            g.load_gavg(sp, gavg_in)
            sp.dma_start(wraw[:, 0, :], w3[0]).then_inc(w_in[0], 16)
            g.load(sp, xt, 0, 1)
            sp.dma_start(wraw[:, 1, :], w3[1]).then_inc(w_in[1], 16)
            for j in range(2, NT):
                sp.dma_start(wraw[:, j, :], w3[j]).then_inc(w_in[j], 16)
            sp.dma_start(woraw[:], wo).then_inc(wo_in, 16)
            for dst, src in ((g.cols[:], cols_in), (g.ident[:], ident_in), (g.sign[:], sign_in),
                             (g.sin_sb[0:HD, :], sin_in), (g.sin_sb[HD:P, :], sin_in),
                             (g.cos_sb[0:HD, :], cos_in), (g.cos_sb[HD:P, :], cos_in)):
                sp.dma_start(dst, src).then_inc(g.s_const, 16)

        @block.gpsimd
        def _(pool):
            for j in range(NT):
                if j == 2:
                    for c in range(NT):
                        g.apply(pool, 0, c)
                pool.wait_ge(w_lo, j + 1)
                pool.dma_start(w_scr[j], wsplit[:, j]).then_inc(w_out, 16)
                if j < 2:
                    pool.dma_start(w_scr[NT + j], wsplit[:, j]).then_inc(w_out, 16)
            pool.wait_ge(w_out, 16 * (NT + 2))

        @block.scalar
        def _(act):
            def weights_high(j):
                act.wait_ge(w_in[j], 16)
                nc.scalar.activation(wsplit[:, j, :, 0, :], wraw[:, j, :].rearrange("p (k o) -> p k o", o=P),
                                     ACT.Copy, scale=W_SCALE).then_inc(w_hi, 1)

            weights_high(0)
            weights_high(1)
            act.wait_ge(eps_ok, 1)
            g.root(act, 0)
            for c in range(NT):
                g.high(act, 0, c)
            for j in range(2, NT):
                weights_high(j)
            act.wait_ge(wo_in, 16)
            nc.scalar.activation(g.wo_sb[:, :, 0, :], woraw[:], ACT.Copy, scale=W_SCALE).then_inc(w_hi, 1)

        @block.tensor
        def _(pe):
            for what in range(2):
                g.average(pe, 0, what)

        @block.vector
        def _(dve):
            def weights_low(j):
                dve.wait_ge(w_hi, j + 1)
                nc.vector.scalar_tensor_tensor(
                    wsplit[:, j, :, 1, :], wraw[:, j, :].rearrange("p (k o) -> p k o", o=P), W_SCALE,
                    wsplit[:, j, :, 0, :], ALU.mult, ALU.subtract).then_inc(w_lo, 1)

            dve.sem_inc(g.small, FREE)
            nc.vector.memset(g.eps[:], GN_EPS).then_inc(eps_ok, 1)
            for c in range(NT):
                if c % 3 == 0:
                    dve.wait_ge(g.x_in[c // 3], 16)
                g.stats(dve, c, g.xraw[:, c, :])
            g.aggregate(dve, 0)
            weights_low(0)
            g.deviations(dve, 0)
            weights_low(1)
            g.scale_shift(dve, 0)
            for c in range(NT):
                g.low(dve, 0, c)
            for j in range(2, NT):
                weights_low(j)
            dve.wait_ge(w_hi, NT + 1)
            nc.vector.scalar_tensor_tensor(g.wo_sb[:, :, 1, :], woraw[:], W_SCALE, g.wo_sb[:, :, 0, :],
                                           ALU.mult, ALU.subtract).then_inc(w_lo, 1)


def main(nc, g, xt, mask, gavg_in, out, w_scr):
    fp32, fp16 = FP32, FP16
    cols, sin_sb, cos_sb, sign, ident = g.cols, g.sin_sb, g.cos_sb, g.sign, g.ident
    wo_sb, xn, kq, kq_swap, v_sb, pj, s_const = g.wo_sb, g.xn, g.kq, g.kq_swap, g.v_sb, g.pj, g.s_const
    with ExitStack() as ctx:
        def sb(name, shape, dt):
            return ctx.enter_context(nc.sbuf_tensor(name, shape, dt))

        def pb(name, shape, dt):
            return ctx.enter_context(nc.psum_tensor(name, shape, dt))

        def sem(name):
            return ctx.enter_context(nc.semaphore(name))

        pbias = sb("pbias", [P, NT, 3], fp32)
        biases = sb("biases", [P, 3], fp32)
        w_sb = sb("w_sb", [P, 3, NT, 2, P], fp16)
        kq_hi = sb("kq_hi", [P, 2, L], fp16)
        kq_lo = sb("kq_lo", [P, 2, L], fp16)
        q_stack = sb("q_stack", [P, 2, L], fp16)
        k_hihi = sb("k_hihi", [P, 2, L], fp16)
        k_lolo = sb("k_lolo", [P, 2, L], fp16)
        v_nat = sb("v_nat", [P, NK, 2, 2, HD], fp16)
        mask_sb = sb("mask_sb", [P, 4, L], fp32)
        neg = sb("neg", [P, 2, L], fp32)
        neg_max = sb("neg_max", [P, NQ], fp32)
        rowsum = sb("rowsum", [P, NQ], fp32)
        rowrec = sb("rowrec", [P, NQ], fp32)
        prob = sb("prob", [P, 2, L], fp32)
        pt_hi = sb("pt_hi", [P, 2, L], fp16)
        pt_lo = sb("pt_lo", [P, 2, L], fp16)
        o_hi = sb("o_hi", [P, 2, 4, HD], fp32)
        o_sum = sb("o_sum", [P, 4, HD], fp32)
        o_nat = sb("o_nat", [P, NK, P], fp32)
        v_pad = sb("v_pad", [P, PSIDE, PSIDE], fp32)
        dw_cols = sb("dw_cols", [P, NCOL], fp32)
        dw = sb("dw", [P, L], fp32)
        tap = sb("tap", [P, 2, L], fp32)
        dw_all = sb("dw_all", [P, L], fp32)
        o_split = sb("o_split", [P, NT, 2, L], fp16)
        x_res = sb("x_res", [P, 2, HALF], fp32)
        out_sb = sb("out_sb", [P, 2, HALF], fp32)

        ps = pb("ps", [P, 2, 2, HALF], fp32)
        pt = pb("pt", [P, 2, HALF], fp32)
        pv = pb("pv", [P, 4, 2, HD], fp32)

        s_ready = sem("s_ready")
        s_mask = [sem(f"s_mask{n}") for n in range(4)]
        s_wkq = sem("s_wkq")
        s_wv = sem("s_wv")
        s_proj = sem("s_proj")
        s_pev = sem("s_pev")
        s_bias = sem("s_bias")
        s_swap = [sem(f"s_swap{n}") for n in range(2)]
        s_rot = sem("s_rot")
        s_rhi = sem("s_rhi")
        s_rlo = sem("s_rlo")
        s_rcos = sem("s_rcos")
        s_rsin = sem("s_rsin")
        s_kstack = sem("s_kstack")
        s_qstack = sem("s_qstack")
        s_vt = sem("s_vt")
        s_vhi = sem("s_vhi")
        s_vlo = sem("s_vlo")
        s_vpad = sem("s_vpad")
        s_cols = sem("s_cols")
        s_s = sem("s_s")
        s_min = sem("s_min")
        s_exp = sem("s_exp")
        s_t = sem("s_t")
        s_hi = sem("s_hi")
        s_lo = sem("s_lo")
        s_pv = sem("s_pv")
        s_ohi = sem("s_ohi")
        s_rec = sem("s_rec")
        s_osum = sem("s_osum")
        s_on = sem("s_on")
        s_dw = sem("s_dw")
        s_mul = sem("s_mul")
        s_add = sem("s_add")
        s_ot = sem("s_ot")
        s_ota = sem("s_ota")
        s_othi = sem("s_othi")
        s_otlo = sem("s_otlo")
        s_op = sem("s_op")
        s_oev = sem("s_oev")
        s_xs = [sem(f"s_xs{n}") for n in range(2)]
        s_xr = [sem(f"s_xr{n}") for n in range(2)]
        s_res = sem("s_res")
        s_store = [sem(f"s_store{n}") for n in range(2)]
        s_gate = [sem(f"s_gate{n}") for n in range(2)]
        s_stored = sem("s_stored")
        NCONST = 6

        block = ctx.enter_context(nc.Block())

        def steps(eng, step, after):
            with eng.Fori(0, B) as b:
                step(b * NT, b, 0, 1, True, False)
                with eng.Fori(1, NT - 1) as j:
                    step(b * NT + j, b, j, j + 1, False, False)
                step(b * NT + (NT - 1), b, NT - 1, 0, False, True)
                after(b)

        @block.sync
        def _(sp):
            sp.dma_start(w_sb[:, 0:2], w_scr[0, :, 0:2]).then_inc(s_wkq, 16)
            sp.dma_start(w_sb[:, 2], w_scr[0, :, 2]).then_inc(s_wv, 16)

            def swap(p, n):
                sp.wait_ge(s_pev, p * 6 + (2 * n + 2))
                for o in range(2):
                    sp.dma_start(kq_swap[o:P:2, n, :], kq[1 - o:P:2, n, :]).then_inc(s_swap[n], 16)

            def stack_k(p, h):
                sp.wait_ge(s_rlo, p * 2 + 1)
                for r in range(2):
                    for dst, src in ((k_hihi, kq_hi), (k_lolo, kq_lo)):
                        sp.dma_start(dst[r * HD:(r + 1) * HD, h, :],
                                     src[h * HD:(h + 1) * HD, 0, :]).then_inc(s_kstack, 16)

            def stack_q(p):
                sp.wait_ge(s_rlo, p * 2 + 2)
                for h in range(2):
                    for r, src in enumerate((kq_hi, kq_lo)):
                        sp.dma_start(q_stack[r * HD:(r + 1) * HD, h, :],
                                     src[h * HD:(h + 1) * HD, 1, :]).then_inc(s_qstack, 16)

            def residual(b, a):
                sp.dma_start(x_res[:, a % 2, :], xt[b, :, a // 2, a % 2 * HALF:(a % 2 + 1) * HALF]).then_inc(s_xr[a % 2], 16)

            def weights_kq(p, j):
                sp.wait_ge(s_proj, p * 6 + 4)
                sp.dma_start(w_sb[:, 0:2], w_scr[j, :, 0:2]).then_inc(s_wkq, 16)

            for n in range(2):
                swap(0, n)
            weights_kq(0, 1)
            for h in range(2):
                stack_k(0, h)
            stack_q(0)

            def step(t, b, j, jn, first, last):
                late = LATE if last else 0
                x_tile = lambda buf: buf[:].rearrange("p a n -> p (a n)")
                for i in range(NQ):
                    sp.wait_ge(s_min, t * NQ + max(i - 3, 0) + FREE)
                    sp.dma_start(mask_sb[:, i % 4, :], mask[j * 2 + i // NK, i % NK]).then_inc(s_mask[i % 4], 16)
                    if first and i == 4:
                        sp.wait_ge(s_res, b * 2 * NT + FREE)
                        sp.dma_start(x_tile(x_res), xt[b + 1, :, 0, :]).then_inc(s_xs[0], 16)
                        sp.wait_ge(s_stored, b * 2 * NT + FREE)
                        sp.dma_start(x_tile(out_sb), xt[b + 1, :, NT - 1, :]).then_inc(s_xs[1], 16)
                    elif i == 4 and not last:
                        sp.wait_ge(g.bn_ok, (b + 1) * 2 * NT + j * 2 + 2)
                        sp.dma_start(x_tile(x_res), xt[b + 1, :, j, :]).then_inc(s_xs[0], 16)
                    if last and i == 0:
                        g.load_gavg(sp, gavg_in)
                    if last and i in (3, 4):
                        sp.wait_ge(s_proj, t * 6 + 6)
                        g.load(sp, xt, b + 1, i - 3)
                    if i == 3:
                        sp.wait_ge(s_proj, t * 6 + 6)
                        sp.dma_start(w_sb[:, 2], w_scr[jn, :, 2]).then_inc(s_wv, 16)
                    if i == 8 + late:
                        swap(t + 1, 0)
                    if i == 13 and not last:
                        stack_k(t + 1, 0)
                if last:
                    sp.wait_ge(g.bn_ok, (b + 2) * 2 * NT)
                    residual(b, 0)
                    residual(b, 1)
                swap(t + 1, 1)
                weights_kq(t + 1, j + 2)
                sp.wait_ge(s_s, t * NQ + NQ)
                if last:
                    stack_k(t + 1, 0)
                stack_k(t + 1, 1)
                stack_q(t + 1)

            def after(b):
                for a in range(2, 2 * NT):
                    sp.wait_ge(s_res, b * 2 * NT + (a - 1) + FREE)
                    residual(b, a)

            steps(sp, step, after)
            sp.wait_ge(s_kstack, 128 * (B * NT + 1))
            sp.wait_ge(s_qstack, 64 * (B * NT + 1))
            sp.wait_ge(s_wkq, 16 * (B * NT + 2))

        @block.gpsimd
        def _(pool):
            def rotate_sin(p, n):
                pool.wait_ge(s_swap[n], p * 32 + 32)
                nc.gpsimd.tensor_tensor(kq_swap[:, n, :], kq_swap[:, n, :], sin_sb[:], ALU.mult).then_inc(s_rsin, 1)

            pool.wait_ge(s_ready, 4)
            for n in range(2):
                rotate_sin(0, n)

            def step(t, b, j, jn, first, last):
                if not first:
                    pool.wait_ge(s_othi, t + FREE)
                    nc.gpsimd.tensor_tensor(o_split[:, j - 1, 1, :], dw_all[:], o_split[:, j - 1, 0, :],
                                            ALU.subtract).then_inc(s_otlo, 1)
                for k in range(1, POOL_TAPS + 1):
                    if last and k == 2:
                        for c in range(NT):
                            g.apply(pool, b + 1, c)
                    for n in range(2):
                        if k == (10 if last else 5 + 6 * n) and not (last and n == 1):
                            rotate_sin(t + 1, n)
                    n = k if k < DW_AT else k - 1
                    if k == DW_AT:
                        pool.wait_ge(s_dw, t * DVE_TAPS + DVE_TAPS)
                    else:
                        pool.wait_ge(s_mul, t * POOL_TAPS + (n + 1))
                    if k == 1:
                        pool.wait_ge(s_otlo, t + FREE)
                    else:
                        pool.wait_ge(s_add, t * POOL_TAPS + (k - 1) + FREE)
                    nc.gpsimd.tensor_tensor(dw_all[:], tap[:, 0] if k == 1 else dw_all[:],
                                            dw[:] if k == DW_AT else tap[:, n % 2], ALU.add).then_inc(s_add, 1)
                if last:
                    rotate_sin(t + 1, 1)

            def after(b):
                for a in range(2 * NT):
                    pool.wait_ge(s_res, b * 2 * NT + (a + 1) + FREE)
                    pool.sem_inc(s_gate[1], 1)
                    pool.dma_start(out[b, :, a // 2, a % 2 * HALF:(a % 2 + 1) * HALF],
                                   out_sb[:, a % 2, :]).then_inc(s_store[a % 2], 16)
                    if a > 0:
                        pool.wait_ge(s_store[(a - 1) % 2], b * 16 * NT + 16 * ((a - 1) // 2 + 1))
                        pool.sem_inc(s_stored, 1)
                pool.wait_ge(s_store[1], b * 16 * NT + 16 * NT)
                pool.sem_inc(s_stored, 1)

            steps(pool, step, after)

        @block.scalar
        def _(act):
            act.wait_ge(s_ready, 4)

            def own_biases(p, jn):
                nc.scalar.activation(biases[:], pbias[:, jn, :], ACT.Copy).then_inc(s_bias, 1)
                act.wait_ge(s_bias, p + 1)

            def copy_out(p, a):
                act.wait_ge(s_proj, p * 6 + (a + 1))
                n, half = a // 2, slice(a % 2 * HALF, (a % 2 + 1) * HALF)
                nc.scalar.activation(v_sb[:, half] if n == 2 else kq[:, n, half], pj[:],
                                     ACT.Identity, bias=biases[:, n:n + 1],
                                     scale=(HD ** -0.5 if n == 0 else 1.0) / W_SCALE).then_inc(s_pev, 1)

            def rotated_high(p, n):
                act.wait_ge(s_rot, p * 2 + (n + 1))
                nc.scalar.activation(kq_hi[:, n, :], kq[:, n, :], ACT.Copy).then_inc(s_rhi, 1)

            def value_highs(p):
                for h in range(2):
                    act.wait_ge(s_vt, p * 2 + (h + 1))
                    nc.scalar.activation(v_nat[:, 4 * h:4 * h + 4, :, 0, :],
                                         ps[:, 1, h, :].rearrange("p (k h c) -> p k h c", k=4, h=2),
                                         ACT.Copy).then_inc(s_vhi, 1)

            def pad(n):
                nc.scalar.activation(v_pad[:, PAD:PAD + SIDE, PAD:PAD + SIDE],
                                     v_sb[:].rearrange("p (r c) -> p r c", c=SIDE), ACT.Copy).then_inc(s_vpad, 1)

            own_biases(0, 0)
            for a in range(4):
                copy_out(0, a)
            rotated_high(0, 0)
            copy_out(0, 4)
            copy_out(0, 5)
            rotated_high(0, 1)
            value_highs(0)
            act.wait_ge(s_pev, 6)
            pad(0)

            def step(t, b, j, jn, first, last):
                def high(i):
                    for h in range(2):
                        act.wait_ge(s_t, t * 2 * NQ + (2 * i + h + 1) + FREE)
                        if h == 0:
                            act.wait_ge(s_pv, t * NQ + max(i - 1, 0) + FREE)
                        nc.scalar.activation(pt_hi[:, i % 2, h * HALF:(h + 1) * HALF], pt[:, h, :], ACT.Copy,
                                             scale=P_SCALE).then_inc(s_hi, 1)

                def group(g):
                    act.wait_ge(s_pv, t * NQ + 4 * (g + 1) + FREE)
                    nc.scalar.activation(o_hi[:, g % 2], pv[:, :, 0, :], ACT.Copy,
                                         scale=1.0 / P_SCALE).then_inc(s_ohi, 1)

                def tap_products(k):
                    r, c = k // KS, k % KS
                    if k == 0:
                        act.wait_ge(s_cols, t + 1)
                        act.wait_ge(s_vpad, t + 1)
                    act.wait_ge(s_add, t * POOL_TAPS + (max(k - 2, 1) if k > 1 else 0) + FREE)
                    nc.scalar.activation(tap[:, k % 2].rearrange("p (r c) -> p r c", c=SIDE),
                                         v_pad[:, r:r + SIDE, c:c + SIDE], ACT.Identity, scale=dw_cols[:, k:k + 1],
                                         bias=dw_cols[:, COL_LB:COL_LB + 1] if k == 0 else 0.0).then_inc(s_mul, 1)

                def output_high(p, k):
                    act.wait_ge(s_ota, p * 2 + 2 + FREE)
                    nc.scalar.activation(o_split[:, k, 0, :], dw_all[:], ACT.Copy).then_inc(s_othi, 1)

                late = LATE if last else 0
                own_biases(t + 1, jn)
                for i in range(NQ + 5):
                    for a in range(6):
                        if i == 3 * a + 3 + late and not (last and a > 3):
                            copy_out(t + 1, a)
                    if i >= LAG + 5 and (i - LAG - 5) % 4 == 0:
                        group((i - LAG - 5) // 4)
                    for n in range(2):
                        if i == 9 + 6 * n + late and not (last and n == 1):
                            rotated_high(t + 1, n)
                    if LAG <= i < NQ + LAG:
                        high(i - LAG)
                    if i < NQ:
                        act.wait_ge(s_min, t * NQ + (i + 1) + FREE)
                        act.wait_ge(s_t, t * 2 * NQ + max(2 * (i - 1), 0) + FREE)
                        nc.scalar.activation(prob[:, i % 2, :], neg[:, i % 2, :], ACT.Exp, scale=-1.0,
                                             bias=neg_max[:, i:i + 1], accum_out=rowsum[:, i:i + 1]).then_inc(s_exp, 1)
                    if i == 2 and not first:
                        output_high(t - 1, j - 1)
                    if i < 2:
                        tap_products(i)
                    elif last:
                        for k in {4: (2,), 8: (3,), 9: (4,), 10: (5,), 11: (6,), 12: (7,), 13: (8, 9), 14: (10,),
                                  15: (11,), 16: (12,), 17: (13,)}.get(i, ()):
                            tap_products(k)
                    elif 4 <= i < POOL_TAPS:
                        tap_products(i - 2)
                    elif i in (16, 17):
                        tap_products(POOL_TAPS - 18 + i)
                    if last and i == 2:
                        g.root(act, b + 1)
                    if last:
                        for c in {4: (0,), 5: (1, 2), 6: (3, 4), 7: (5,)}.get(i, ()):
                            g.high(act, b + 1, c)
                if last:
                    copy_out(t + 1, 4)
                    output_high(t, j)
                    copy_out(t + 1, 5)
                value_highs(t + 1)
                if last:
                    rotated_high(t + 1, 1)
                act.wait_ge(s_dw, t * DVE_TAPS + DVE_TAPS)
                pad(t)

            def after(b):
                for a in range(2 * NT):
                    m, h = a // 2, a % 2
                    act.wait_ge(s_op, b * 2 * NT + (a + 1))
                    act.wait_ge(s_stored, b * 2 * NT + max(a - 1, 0) + FREE)
                    nc.scalar.activation(out_sb[:, a % 2, :], ps[:, (a // 2) % 2, h, :],
                                         ACT.Identity, bias=cols[:, m, COL_O:COL_O + 1],
                                         scale=1.0 / W_SCALE).then_inc(s_oev, 1)

            steps(act, step, after)

        @block.tensor
        def _(pe):
            TERMS = ((0, 0), (0, 1), (1, 0))
            PER = NT * len(TERMS)

            def project(p, start, stop):
                for x in range(start, stop):
                    a, y = x // PER, x % PER
                    n, h, k = a // 2, a % 2, y // len(TERMS)
                    s, m = TERMS[y % len(TERMS)]
                    if y == 0 and a > 0:
                        pe.wait_ge(s_pev, p * 6 + a)
                    mm = nc.tensor.matmul(pj[:], w_sb[:, n, k, s, :],
                                          xn[:, k, m, h * HALF:(h + 1) * HALF], start=(y == 0), stop=(y == PER - 1))
                    if y == PER - 1:
                        mm.then_inc(s_proj, 1)

            def turn_values(p, first):
                for h in range(2):
                    pe.wait_ge(s_pev, p * 6 + (5 + h))
                    if not first:
                        pe.wait_ge(s_min, p * NQ + FREE)
                    for k in range(4):
                        mm = nc.tensor.transpose(ps[:, 1, h, k * P:(k + 1) * P],
                                                 v_sb[:, h * HALF + k * P:h * HALF + (k + 1) * P], ident[:])
                    mm.then_inc(s_vt, 1)

            pe.wait_ge(s_const, 16 * (NCONST + 1))
            pe.wait_ge(s_wkq, 16)
            pe.wait_ge(s_wv, 16)
            project(0, 0, 6 * PER)
            turn_values(0, True)

            def step(t, b, j, jn, first, last):
                def scores(i):
                    h, q = i // NK, i % NK
                    if i == 0:
                        pe.wait_ge(s_kstack, t * 128 + 128)
                        pe.wait_ge(s_qstack, t * 64 + 64)
                        pe.wait_ge(s_oev, b * 2 * NT + FREE)
                    if i == 1:
                        pe.wait_ge(s_vlo, t * 2 + 2)
                    if i >= 2:
                        pe.wait_ge(s_min, t * NQ + (i - 1) + FREE)
                    for s, k_part in enumerate((k_hihi, k_lolo)):
                        for n in range(2):
                            mm = nc.tensor.matmul(ps[:, i % 2, n, :], q_stack[:, h, q * P:(q + 1) * P],
                                                  k_part[:, h, n * HALF:(n + 1) * HALF], start=(s == 0), stop=(s == 1))
                    mm.then_inc(s_s, 1)

                def transposes(i):
                    pe.wait_ge(s_exp, t * NQ + (i + 1) + FREE)
                    for h in range(2):
                        if i == 0:
                            pe.wait_ge(s_ota, t * 2 + FREE)
                        else:
                            pe.wait_ge(s_lo, t * 2 * NQ + (2 * i - 1 + h))
                        for k in range(4):
                            c = (4 * h + k) * P
                            mm = nc.tensor.transpose(pt[:, h, k * P:(k + 1) * P], prob[:, i % 2, c:c + P], ident[:])
                        mm.then_inc(s_t, 1)

                def values(i):
                    h, g = i // NK, i // 4
                    if i % 4 == 0:
                        pe.wait_ge(s_osum, t * 4 + g + FREE)
                    pe.wait_ge(s_lo, t * 2 * NQ + (2 * i + 2))
                    for k in range(NK):
                        nc.tensor.matmul(pv[:, i % 4].rearrange("p a c -> p (a c)"), pt_hi[:, i % 2, k * P:(k + 1) * P],
                                         v_nat[:, k, h].rearrange("p a c -> p (a c)"), start=(k == 0), stop=False)
                    for k in range(NK):
                        mm = nc.tensor.matmul(pv[:, i % 4, 0, :], pt_lo[:, i % 2, k * P:(k + 1) * P],
                                              v_nat[:, k, h, 0, :], start=False, stop=(k == NK - 1))
                    mm.then_inc(s_pv, 1)

                def turn_outputs(p):
                    pe.wait_ge(s_on, p * 4 + 4)
                    pe.wait_ge(s_lo, p * 2 * NQ + 2 * NQ)
                    for h in range(2):
                        for k in range(4):
                            mm = nc.tensor.transpose(pt[:, h, k * P:(k + 1) * P], o_nat[:, 4 * h + k, :], ident[:])
                        mm.then_inc(s_ot, 1)

                late = LATE if last else 0
                for i in range(NQ + LAG + 1):
                    if i < NQ:
                        scores(i)
                    if i == 1 and not first:
                        turn_outputs(t - 1)
                    if LAG < i < NQ + LAG or i == LAG and last:
                        transposes(i - LAG)
                    if i == 1 and last:
                        pe.wait_ge(s_pev, t * 6 + 6)
                        g.average(pe, b + 1, 0)
                    if i == 2 and last:
                        g.average(pe, b + 1, 1)
                    if i == late:
                        pe.wait_ge(s_wkq, t * 16 + 32)
                        pe.wait_ge(s_pev, t * 6 + 6)
                    if last and late <= i < late + 3:
                        pe.wait_ge(g.xlo_ok, (b + 1) * NT + 2 * (i - late + 1))
                    if i == 12 and not last:
                        pe.wait_ge(s_wv, t * 16 + 32)
                    start = (i - late) * PER // 3
                    here = late <= i < late + (12 if last else 18)
                    values_first = start % PER == 0 and (i == LAG + 1 or i % 4 != 3)
                    if LAG < i and values_first:
                        values(i - LAG - 1)
                    if here:
                        project(t + 1, start, start + PER // 3)
                    if i == LAG and not last:
                        transposes(0)
                    if LAG < i and not values_first:
                        values(i - LAG - 1)
                if last:
                    pe.wait_ge(s_wv, t * 16 + 32)
                    project(t + 1, 4 * PER, 5 * PER)
                    turn_outputs(t)
                    project(t + 1, 5 * PER, 6 * PER)
                turn_values(t + 1, False)

            def after(b):
                pe.wait_ge(s_otlo, b * NT + NT + FREE)
                pe.wait_ge(s_pev, b * 6 * NT + 6 * (NT + 1))
                for a in range(2 * NT):
                    m, h = a // 2, a % 2
                    if a == 2:
                        pe.wait_ge(s_vlo, b * 2 * NT + 2 * (NT + 1))
                    if a >= 4:
                        pe.wait_ge(s_oev, b * 2 * NT + (a - 3) + FREE)
                    for k in range(NT):
                        for s, r in TERMS:
                            mm = nc.tensor.matmul(ps[:, m % 2, h, :], wo_sb[:, k, s, m * P:(m + 1) * P],
                                                  o_split[:, k, r, h * HALF:(h + 1) * HALF],
                                                  start=(k == 0 and (s, r) == TERMS[0]),
                                                  stop=(k == NT - 1 and (s, r) == TERMS[-1]))
                    mm.then_inc(s_op, 1)

            steps(pe, step, after)

        @block.vector
        def _(dve):
            for free in (s_min, s_res, s_pv, s_t, s_oev, s_ota, s_osum, s_exp, s_othi, s_otlo, s_stored, s_add):
                dve.sem_inc(free, FREE)
            nc.vector.memset(v_pad[:], 0.0).then_inc(s_ready, 1)
            dve.wait_ge(s_const, 16 * (NCONST + 1))
            nc.vector.tensor_scalar(pbias[:, :, 0], cols[:, :, COL_K], HD ** -0.5, None, ALU.mult).then_inc(s_ready, 1)
            nc.vector.tensor_copy(pbias[:, :, 1:3], cols[:, :, COL_Q:COL_V + 1]).then_inc(s_ready, 1)
            nc.vector.tensor_scalar(sin_sb[:], sin_sb[:], sign[:, 0:1], None, ALU.mult).then_inc(s_ready, 1)
            dve.wait_ge(s_ready, 4)

            def rotate_cos(p, n):
                dve.wait_ge(s_swap[n], p * 32 + 32)
                nc.vector.tensor_tensor(kq[:, n, :], kq[:, n, :], cos_sb[:], ALU.mult).then_inc(s_rcos, 1)

            def rotate_sum(p, n):
                dve.wait_ge(s_rcos, p * 2 + (n + 1))
                dve.wait_ge(s_rsin, p * 2 + (n + 1))
                nc.vector.tensor_tensor(kq[:, n, :], kq[:, n, :], kq_swap[:, n, :], ALU.add).then_inc(s_rot, 1)

            def rotated_low(p, n):
                dve.wait_ge(s_rhi, p * 2 + (n + 1))
                nc.vector.tensor_tensor(kq_lo[:, n, :], kq[:, n, :], kq_hi[:, n, :], ALU.subtract).then_inc(s_rlo, 1)

            def value_lows(p):
                for h in range(2):
                    dve.wait_ge(s_vhi, p * 2 + (h + 1))
                    nc.vector.tensor_tensor(v_nat[:, 4 * h:4 * h + 4, :, 1, :],
                                            ps[:, 1, h, :].rearrange("p (k h c) -> p k h c", k=4, h=2),
                                            v_nat[:, 4 * h:4 * h + 4, :, 0, :], ALU.subtract).then_inc(s_vlo, 1)

            for n in range(2):
                rotate_cos(0, n)
                rotate_sum(0, n)
                rotated_low(0, n)
            value_lows(0)

            def step(t, b, j, jn, first, last):
                done = [0]

                image = dw[:].rearrange("p (r c) -> p r c", c=SIDE)

                def taps(n):
                    for _ in range(n):
                        k = done[0]
                        if k >= DVE_TAPS:
                            return
                        w = POOL_TAPS + k
                        r, c = w // KS, w % KS
                        src = v_pad[:, r:r + SIDE, c:c + SIDE]
                        if k == 0:
                            dve.wait_ge(s_vpad, t + 1)
                            dve.wait_ge(s_cols, t + 1)
                            dve.wait_ge(s_add, t * POOL_TAPS + FREE)
                            ins = nc.vector.tensor_scalar(image, src, dw_cols[:, w:w + 1], None, ALU.mult)
                        else:
                            dve.wait_ge(s_dw, t * DVE_TAPS + k)
                            ins = nc.vector.scalar_tensor_tensor(image, src, dw_cols[:, w:w + 1], image,
                                                                 ALU.mult, ALU.add)
                        ins.then_inc(s_dw, 1)
                        done[0] += 1

                def low(i):
                    for h in range(2):
                        dve.wait_ge(s_hi, t * 2 * NQ + (2 * i + h + 1))
                        nc.vector.scalar_tensor_tensor(pt_lo[:, i % 2, h * HALF:(h + 1) * HALF], pt[:, h, :], P_SCALE,
                                                       pt_hi[:, i % 2, h * HALF:(h + 1) * HALF],
                                                       ALU.mult, ALU.subtract).then_inc(s_lo, 1)

                def group(g):
                    h = g // 2
                    dve.wait_ge(s_ohi, t * 4 + (g + 1))
                    nc.vector.reciprocal(rowrec[:, 4 * g:4 * g + 4], rowsum[:, 4 * g:4 * g + 4]).then_inc(s_rec, 1)
                    nc.vector.scalar_tensor_tensor(o_sum[:], pv[:, :, 1, :], 1.0 / P_SCALE, o_hi[:, g % 2],
                                                   ALU.mult, ALU.add).then_inc(s_osum, 1)
                    dve.wait_ge(s_rec, t * 4 + (g + 1))
                    dve.wait_ge(s_osum, t * 4 + (g + 1) + FREE)
                    nc.vector.tensor_tensor(o_nat[:, 4 * (g % 2):4 * (g % 2) + 4, h * HD:(h + 1) * HD], o_sum[:],
                                            rowrec[:, 4 * g:4 * g + 4].unsqueeze(2).to_broadcast([P, 4, HD]),
                                            ALU.mult).then_inc(s_on, 1)

                def output_sum(p):
                    for h in range(2):
                        dve.wait_ge(s_ot, p * 2 + (h + 1))
                        if h == 0:
                            dve.wait_ge(s_add, (p + 1) * POOL_TAPS + FREE)
                        nc.vector.tensor_tensor(dw_all[:, h * HALF:(h + 1) * HALF], pt[:, h, :],
                                                dw_all[:, h * HALF:(h + 1) * HALF], ALU.add).then_inc(s_ota, 1)

                def output_low(p, k):
                    dve.wait_ge(s_othi, p + 1 + FREE)
                    nc.vector.tensor_tensor(o_split[:, k, 1, :], dw_all[:], o_split[:, k, 0, :],
                                            ALU.subtract).then_inc(s_otlo, 1)

                late = LATE if last else 0
                nc.vector.tensor_copy(dw_cols[:], cols[:, j, :]).then_inc(s_cols, 1)
                for i in range(NQ + 5):
                    if i >= LAG + 5 and (i - LAG - 5) % 4 == 0:
                        group((i - LAG - 5) // 4)
                    if i < NQ:
                        dve.wait_ge(s_s, t * NQ + (i + 1))
                        dve.wait_ge(s_exp, t * NQ + max(i - 1, 0) + FREE)
                        dve.wait_ge(s_mask[i % 4], t * 64 + 16 * (i // 4 + 1))
                        dve.sem_inc(s_gate[0], 1)
                        nc.vector.tensor_tensor_reduce(out=neg[:, i % 2, :], in0=ps[:, i % 2].rearrange("p a n -> p (a n)"),
                                                       in1=mask_sb[:, i % 4, :], scale=-1.0, scalar=BIG, op0=ALU.add,
                                                       op1=ALU.min, accum_out=neg_max[:, i:i + 1]).then_inc(s_min, 1)
                    if last and i == 3:
                        g.scale_shift(dve, b + 1)
                    if LAG <= i < NQ + LAG:
                        low(i - LAG)
                    if i == 1 and not first:
                        output_sum(t - 1)
                    if last:
                        if i == 0:
                            g.aggregate(dve, b + 1)
                        if i == 1:
                            g.deviations(dve, b + 1)
                        for c in {5: (0,), 6: (1, 2), 7: (3, 4), 8: (5,)}.get(i, ()):
                            g.low(dve, b + 1, c)
                        taps({0: 1, 2: 1, 3: 1, 4: 1, 8: 1, 9: 2, 10: 1, 11: 1, 12: 1, 13: 1}.get(i, 0))
                    else:
                        taps({0: 2, 2: 1, 3: 1, 4: 1, 5: 1, 6: 1, 8: 1, 9: 1, 11: 1, 12: 1}.get(i, 0))
                        if i == 17:
                            dve.wait_ge(s_xs[0], b * 16 * (NT - 1) + j * 16 + 16)
                            if first:
                                dve.wait_ge(g.small, (b + 1) * g.SMALL + FREE)
                            g.stats(dve, j, x_res[:].rearrange("p a n -> p (a n)"))
                            if first:
                                dve.wait_ge(s_xs[1], b * 16 + 16)
                                g.stats(dve, NT - 1, out_sb[:].rearrange("p a n -> p (a n)"))
                    for n in range(1 if last else 2):
                        if i == 7 + 6 * n + late:
                            rotate_cos(t + 1, n)
                        if i == 8 + 6 * n + late:
                            rotate_sum(t + 1, n)
                        if i == 10 + 5 * n + late:
                            rotated_low(t + 1, n)
                if last:
                    output_sum(t)
                    output_low(t, j)
                value_lows(t + 1)
                if last:
                    rotate_cos(t + 1, 1)
                    rotate_sum(t + 1, 1)
                    rotated_low(t + 1, 1)

            def after(b):
                for a in range(2 * NT):
                    m, h = a // 2, a % 2
                    dve.wait_ge(s_oev, b * 2 * NT + (a + 1) + FREE)
                    dve.wait_ge(s_xr[a % 2], b * 16 * NT + 16 * (a // 2 + 1))
                    nc.vector.tensor_tensor(out_sb[:, a % 2, :], out_sb[:, a % 2, :], x_res[:, a % 2, :],
                                            ALU.add).then_inc(s_res, 1)

            steps(dve, step, after)


def kernel(**inputs):
    import numpy as np
    import concourse.bacc as bacc
    from concourse.bass_utils import run_bass_kernel_spmd

    a = {k.removeprefix("L0_conv_"): np.asarray(v) for k, v in inputs.items()}
    tiles = lambda w: w.reshape(NT, P, NT, P).transpose(0, 3, 2, 1)
    lanes = lambda v: v.reshape(NT, P).T
    f = np.float32
    arrays = {
        "xt": np.concatenate([a["x"], a["x"][:1]]).reshape(B + 1, L, NT, P).transpose(0, 3, 2, 1),
        "w3": np.stack([tiles(a["wk"]), tiles(a["wq"]), tiles(a["wv"])], axis=2).reshape(NT, P, 3 * NT * P),
        "wo": a["wo"].T.reshape(NT, P, C).transpose(1, 0, 2),
        "cols": np.stack([lanes(t) for t in a["lepe_w"].reshape(TAPS, C)]
                         + [lanes(a[n]) for n in ("lepe_b", "bk", "bq", "bv", "bo")], axis=2),
        "mask": a["mask"].reshape(NH, NK, P, L),
        "sin": a["sin"].reshape(L, HD).T,
        "cos": a["cos"].reshape(L, HD).T,
        "ident": np.eye(P, dtype=f),
        "gavg": (np.equal.outer(np.arange(3 * P) // (C // GROUPS), np.arange(3 * P) // (C // GROUPS)).astype(f)
                 * f(GROUPS / C)).reshape(3, P, 3 * P).transpose(1, 0, 2),
        "sign": np.where(np.arange(P) % 2 == 0, -1, 1).astype(f).reshape(P, 1),
    }
    arrays = {k: np.ascontiguousarray(v) for k, v in arrays.items()}
    nc = bacc.Bacc("TRN2", target_bir_lowering=False, num_devices=1)
    fp32, fp16 = mybir.dt.float32, mybir.dt.float16
    d = {k: nc.dram_tensor(f"{k}_in", v.shape, fp32, kind="ExternalInput").ap() for k, v in arrays.items()}
    out = nc.dram_tensor("out_t", (B, P, NT, L), fp32, kind="ExternalOutput").ap()
    w_scr = nc.dram_tensor("w_scr", (NT + 2, P, 3, NT, 2, P), fp16, kind="Internal").ap()
    conv_preact(nc, d["xt"], d["w3"], d["wo"], d["cols"], d["mask"], d["sin"], d["cos"], d["ident"], d["gavg"],
                d["sign"], out, w_scr)
    r = run_bass_kernel_spmd(nc, [{f"{k}_in": v for k, v in arrays.items()}], core_ids=[0])
    got = r.results[0]["out_t"]
    return np.ascontiguousarray(got.transpose(0, 3, 2, 1)).reshape(B, SIDE, SIDE, C)
```
